# Optimizing a Trainium2 kernel written in Bass

```python
import numpy as np
import jax
import jax.numpy as jnp

def _softmax(x, axis=-1):
    return jax.nn.softmax(x, axis=axis)

def _gelu(x):
    return jax.nn.gelu(x, approximate=True)

def _silu(x):
    return jax.nn.silu(x)

def _sigmoid(x):
    return jax.nn.sigmoid(x)

def _layernorm(x, axis=-1, eps=1e-05):
    m = jnp.mean(x, axis=axis, keepdims=True)
    v = jnp.var(x, axis=axis, keepdims=True)
    return (x - m) / jnp.sqrt(v + eps)

def _scatter_add(tgt, idx, src, axis=0):
    return tgt.at[idx].add(src)

def _segment_sum(src, seg, n):
    return jax.ops.segment_sum(src, seg, n)
kernel_name = 'mk_adj_resnorm_d2_adj_r2_864c64'

def setup_inputs(seed: int=0):
    np.random.seed(seed)
    _w = jnp.asarray

    def _rec_inputs():
        import jax
        import jax.numpy as jnp
        _gk = jax.random.key(seed)
        x = -1.56e-05 + 0.05755 * jax.random.normal(jax.random.fold_in(_gk, 1), (16, 512, 128), jnp.float32)
        _a = jax.random.bernoulli(jax.random.fold_in(_gk, 2), 0.03125, (16, 512, 512))
        _a = jnp.logical_or(_a, jnp.swapaxes(_a, -1, -2))
        _a = jnp.logical_or(_a, jnp.eye(512, dtype=bool))
        _af = _a.astype(jnp.float32)
        _af = _af * jax.random.uniform(jax.random.fold_in(_gk, 3), (16, 512, 512), jnp.float32, 0.05, 0.00012207)
        adj = _af
        return (x, adj)
    x, adj = _rec_inputs()

    def _L0_gnn_setup():
        import jax, jax.numpy as jnp
        import numpy as np
        C = 1.0
        SQRT_C = jnp.float32(np.sqrt(C))
        MIN_NORM = 1e-15
        BALL_EPS = 0.004

        def _norm(x):
            return jnp.clip(jnp.linalg.norm(x, axis=-1, keepdims=True), MIN_NORM, None)

        def _artanh(x):
            return jnp.arctanh(jnp.clip(x, -1 + 1e-07, 1 - 1e-07))

        def logmap0(x):
            n = _norm(x)
            return _artanh(SQRT_C * n) * x / (SQRT_C * n)

        def expmap0(u):
            n = _norm(u)
            return jnp.tanh(SQRT_C * n) * u / (SQRT_C * n)

        def project(x):
            n = _norm(x)
            maxnorm = (1.0 - BALL_EPS) / SQRT_C
            return jnp.where(n > maxnorm, x * (maxnorm / n), x)
        key = jax.random.key(seed)
        k1, k2 = jax.random.split(key)
        B, N, D = (2, 4096, 128)
        x = project(expmap0(0.1 * jax.random.normal(k1, (B, N, D), dtype=jnp.float32)))
        adj = jax.random.uniform(k2, (B, N, N), dtype=jnp.float32) / N
        return {'x': x, 'adj': adj}
    _L0_gnn_all = _L0_gnn_setup()
    _L0_gnn_in = {k: v for k, v in _L0_gnn_all.items() if k in ()}
    del _L0_gnn_all

    def _L1_gnn_setup():
        import jax, jax.numpy as jnp
        import numpy as np
        from jax import lax
        DIM = 128
        EPS = 1e-05

        def _bn(h, g, b, m, v):
            scale = g / jnp.sqrt(v + EPS)
            return h * scale[None, :, None] + (b - m * scale)[None, :, None]

        def _conv1d(h, w, pad):
            return lax.conv_general_dilated(h, w, window_strides=(1,), padding=[(pad, pad)], dimension_numbers=('NCH', 'OIH', 'NCH'))
        key = jax.random.key(seed)
        ks = jax.random.split(key, 16)
        bs, n, d = (16, 1024, DIM)
        s = 0.05
        return {'x': jax.random.normal(ks[0], (bs, n, d), jnp.float32), 'mask': jnp.ones((bs, n, n), jnp.float32), 'w_se': jax.random.normal(ks[1], (3, d), jnp.float32) * s, 'b_se': jnp.zeros((3,), jnp.float32), 'conv1_w': jax.random.normal(ks[2], (d, d, 1), jnp.float32) * s, 'bn1_g': jnp.ones((d,), jnp.float32), 'bn1_b': jnp.zeros((d,), jnp.float32), 'bn1_m': jnp.zeros((d,), jnp.float32), 'bn1_v': jnp.ones((d,), jnp.float32), 'conv2_w': jax.random.normal(ks[3], (d, d, 17), jnp.float32) * s, 'bn2_g': jnp.ones((d,), jnp.float32), 'bn2_b': jnp.zeros((d,), jnp.float32), 'bn2_m': jnp.zeros((d,), jnp.float32), 'bn2_v': jnp.ones((d,), jnp.float32), 'w_msg': jax.random.normal(ks[4], (d, d), jnp.float32) * s, 'b_msg': jnp.zeros((d,), jnp.float32), 'w_ih': jax.random.normal(ks[5], (3 * d, 2 * d), jnp.float32) * s, 'b_ih': jnp.zeros((3 * d,), jnp.float32), 'w_hh': jax.random.normal(ks[6], (3 * d, d), jnp.float32) * s, 'b_hh': jnp.zeros((3 * d,), jnp.float32)}
    _L1_gnn_all = _L1_gnn_setup()
    _L1_gnn_in = {k: v for k, v in _L1_gnn_all.items() if k in ('w_se', 'b_se', 'conv1_w', 'bn1_g', 'bn1_b', 'bn1_m', 'bn1_v', 'conv2_w', 'bn2_g', 'bn2_b', 'bn2_m', 'bn2_v', 'w_msg', 'b_msg', 'w_ih', 'b_ih', 'w_hh', 'b_hh')}
    del _L1_gnn_all
    return {'x': x, 'adj': adj, 'L1_gnn_w_se': _L1_gnn_in['w_se'], 'L1_gnn_b_se': _L1_gnn_in['b_se'], 'L1_gnn_conv1_w': _L1_gnn_in['conv1_w'], 'L1_gnn_bn1_g': _L1_gnn_in['bn1_g'], 'L1_gnn_bn1_b': _L1_gnn_in['bn1_b'], 'L1_gnn_bn1_m': _L1_gnn_in['bn1_m'], 'L1_gnn_bn1_v': _L1_gnn_in['bn1_v'], 'L1_gnn_conv2_w': _L1_gnn_in['conv2_w'], 'L1_gnn_bn2_g': _L1_gnn_in['bn2_g'], 'L1_gnn_bn2_b': _L1_gnn_in['bn2_b'], 'L1_gnn_bn2_m': _L1_gnn_in['bn2_m'], 'L1_gnn_bn2_v': _L1_gnn_in['bn2_v'], 'L1_gnn_w_msg': _L1_gnn_in['w_msg'], 'L1_gnn_b_msg': _L1_gnn_in['b_msg'], 'L1_gnn_w_ih': _L1_gnn_in['w_ih'], 'L1_gnn_b_ih': _L1_gnn_in['b_ih'], 'L1_gnn_w_hh': _L1_gnn_in['w_hh'], 'L1_gnn_b_hh': _L1_gnn_in['b_hh']}

def reference(x, adj, L1_gnn_w_se, L1_gnn_b_se, L1_gnn_conv1_w, L1_gnn_bn1_g, L1_gnn_bn1_b, L1_gnn_bn1_m, L1_gnn_bn1_v, L1_gnn_conv2_w, L1_gnn_bn2_g, L1_gnn_bn2_b, L1_gnn_bn2_m, L1_gnn_bn2_v, L1_gnn_w_msg, L1_gnn_b_msg, L1_gnn_w_ih, L1_gnn_b_ih, L1_gnn_w_hh, L1_gnn_b_hh):
    import jax
    import jax.numpy as jnp

    def _L0_gnn_ref(x, adj):
        import jax, jax.numpy as jnp
        import numpy as np
        C = 1.0
        SQRT_C = jnp.float32(np.sqrt(C))
        MIN_NORM = 1e-15
        BALL_EPS = 0.004

        def _norm(x):
            return jnp.clip(jnp.linalg.norm(x, axis=-1, keepdims=True), MIN_NORM, None)

        def _artanh(x):
            return jnp.arctanh(jnp.clip(x, -1 + 1e-07, 1 - 1e-07))

        def logmap0(x):
            n = _norm(x)
            return _artanh(SQRT_C * n) * x / (SQRT_C * n)

        def expmap0(u):
            n = _norm(u)
            return jnp.tanh(SQRT_C * n) * u / (SQRT_C * n)

        def project(x):
            n = _norm(x)
            maxnorm = (1.0 - BALL_EPS) / SQRT_C
            return jnp.where(n > maxnorm, x * (maxnorm / n), x)
        x_tangent = logmap0(x)
        support_t = jnp.einsum('bij,bjd->bid', adj, x_tangent)
        return project(expmap0(support_t))

    def _L1_gnn_ref(x, mask, w_se, b_se, conv1_w, bn1_g, bn1_b, bn1_m, bn1_v, conv2_w, bn2_g, bn2_b, bn2_m, bn2_v, w_msg, b_msg, w_ih, b_ih, w_hh, b_hh):
        import jax, jax.numpy as jnp
        import numpy as np
        from jax import lax
        DIM = 128
        EPS = 1e-05

        def _bn(h, g, b, m, v):
            scale = g / jnp.sqrt(v + EPS)
            return h * scale[None, :, None] + (b - m * scale)[None, :, None]

        def _conv1d(h, w, pad):
            return lax.conv_general_dilated(h, w, window_strides=(1,), padding=[(pad, pad)], dimension_numbers=('NCH', 'OIH', 'NCH'))
        d = x.shape[-1]
        xc = jnp.transpose(x, (0, 2, 1))
        h = _bn(_conv1d(xc, conv1_w, 0), bn1_g, bn1_b, bn1_m, bn1_v)
        h = jax.nn.relu(h)
        h = _bn(_conv1d(h, conv2_w, 8), bn2_g, bn2_b, bn2_m, bn2_v)
        x_conv = jnp.transpose(jax.nn.relu(h + xc), (0, 2, 1))
        s = x @ w_se.T + b_se
        sq = jnp.sum(s * s, axis=-1)
        dist = sq[:, :, None] + sq[:, None, :] - 2.0 * jnp.einsum('bnd,bmd->bnm', s, s)
        A = jnp.exp(-dist) * mask
        msg = jax.nn.relu(x @ w_msg.T + b_msg)
        x_nmp = jnp.einsum('bnm,bmd->bnd', A, msg)
        x_in = jnp.concatenate([x_conv, x_nmp], axis=-1)
        gi = x_in @ w_ih.T + b_ih
        gh = x @ w_hh.T + b_hh
        gi_r, gi_z, gi_n = (gi[..., :d], gi[..., d:2 * d], gi[..., 2 * d:])
        gh_r, gh_z, gh_n = (gh[..., :d], gh[..., d:2 * d], gh[..., 2 * d:])
        r = jax.nn.sigmoid(gi_r + gh_r)
        z = jax.nn.sigmoid(gi_z + gh_z)
        nn_ = jnp.tanh(gi_n + r * gh_n)
        return (1.0 - z) * nn_ + z * x
    x = _layernorm(x + _L0_gnn_ref(x, adj), axis=-1)
    x = _layernorm(x + _L1_gnn_ref(x, adj, L1_gnn_w_se, L1_gnn_b_se, L1_gnn_conv1_w, L1_gnn_bn1_g, L1_gnn_bn1_b, L1_gnn_bn1_m, L1_gnn_bn1_v, L1_gnn_conv2_w, L1_gnn_bn2_g, L1_gnn_bn2_b, L1_gnn_bn2_m, L1_gnn_bn2_v, L1_gnn_w_msg, L1_gnn_b_msg, L1_gnn_w_ih, L1_gnn_b_ih, L1_gnn_w_hh, L1_gnn_b_hh), axis=-1)
    return x

_drawn_inputs = setup_inputs


def setup_inputs(seed=0):
    import zlib

    import numpy as np

    out = dict(_drawn_inputs(seed))
    spreads = {'L1_gnn_b_se': (0.0, 2.0),
     'L1_gnn_bn1_g': (1.0, 0.6),
     'L1_gnn_bn1_b': (0.0, 0.412),
     'L1_gnn_bn1_m': (0.0, 0.373),
     'L1_gnn_bn1_v': (1.0, 0.6),
     'L1_gnn_bn2_g': (1.0, 0.571),
     'L1_gnn_bn2_b': (0.0, 0.73),
     'L1_gnn_bn2_m': (0.0, 0.563),
     'L1_gnn_bn2_v': (1.0, 0.6),
     'L1_gnn_b_msg': (0.0, 2.0),
     'L1_gnn_b_ih': (0.0, 0.267),
     'L1_gnn_b_hh': (0.0, 0.393)}
    factors = {'L1_gnn_w_se': 57.944, 'L1_gnn_w_msg': 21.443}
    for name, (base, spread) in spreads.items():
        noise = np.random.default_rng([zlib.crc32(name.encode()), seed]).standard_normal(out[name].shape)
        drawn = base * np.exp(spread * noise) if base else spread * noise
        out[name] = jnp.asarray(drawn.astype(out[name].dtype))
    for name, factor in factors.items():
        out[name] = (out[name] * factor).astype(out[name].dtype)
    return out
```

```python
from contextlib import ExitStack

import numpy as np

import concourse.bass as bass
from concourse import mybir

F32 = mybir.dt.float32
F32R = mybir.dt.float32r
ALU = mybir.AluOpType
ACT = mybir.ActivationFunctionType
AX = mybir.AxisListType

B, N, D = 16, 512, 128
T = N // 128
SE = 3
TAPS = 17
PAD = TAPS // 2
HT = (TAPS + 1) // 2
HALF = N // 2
HW = HALF + PAD
EPS = 1e-5
MIN_NORM = 1e-15
MAX_NORM = 1.0 - 0.004
ARTANH_MAX = float(np.float32(1 - 1e-07))
SERIES_BELOW = 0.25
SERIES = [1.0 / (2 * k + 1) for k in range(8)]

(V_G1, V_B1, V_M1, V_V1, V_G2, V_B2, V_M2, V_V2, V_IR, V_IZ, V_IN, V_HR, V_HZ, V_HN, V_SE) = range(15)
N_VEC = 15
(C_MU, C_NU, C_AA, C_BA, C_CA, C_AB, C_BB, C_CB) = range(8)
(W_SC1, W_BI1, W_SC2, W_BI2, W_HR, W_HZ, W_N, W_HHN, W_NU, W_T1, W_T2, W_T3, W_T4) = range(13)


def distance_rows():
    c = np.zeros((128, 8), np.float32)
    for p in range(128):
        group, row = p // 32, p % 32
        kind = row // SE if row < 3 * SE else 3
        low_a, low_b = group >= 2, group % 2 == 1
        c[p, C_MU] = kind in (1, 2)
        c[p, C_NU] = kind not in (1, 2)
        c[p, C_AA] = kind != 1
        c[p, C_BA] = -0.25 if kind == 1 else 0.0
        c[p, C_CA] = -1.0 if low_a and kind != 1 else 0.0
        c[p, C_AB] = kind != 2
        c[p, C_BB] = -0.25 if kind == 2 else 0.0
        c[p, C_CB] = -1.0 if low_b and kind != 2 else 0.0
    return c


def build(nc, x, adj_t, w_conv2, w_gru, w_small, vectors, b_msg, rows_const, ident_in, out):
    with ExitStack() as ctx:
        def sem(name):
            return ctx.enter_context(nc.semaphore(name))

        def sb(name, shape, dt=F32, where=ctx):
            return where.enter_context(nc.sbuf_tensor(name, shape, dt))

        def psum(name):
            return ctx.enter_context(nc.psum_tensor(name, [128, 512], F32))

        bank_a = [psum("bank_a0"), psum("bank_a1")]
        bank_c = psum("bank_c")
        bank_p = psum("bank_p")
        bank_x = psum("bank_x")
        bank_y = psum("bank_y")
        bank_w = psum("bank_w")
        bank_v = psum("bank_v")

        adj_sb = [sb(f"adj_sb{i}", [128, T, N]) for i in range(2)]
        adj_hi = sb("adj_hi", [128, T, N], F32R)
        adj_lo = sb("adj_lo", [128, T, N], F32R)
        conv_hi = sb("conv_hi", [128, 3, HT, 128], F32R)
        conv_lo = sb("conv_lo", [128, 3, HT, 128], F32R)
        gru_hi = sb("gru_hi", [128, 9, 128], F32R)
        gru_lo = sb("gru_lo", [128, 9, 128], F32R)
        small_hi = sb("small_hi", [128, 3, 128], F32R)
        small_lo = sb("small_lo", [128, 3, 128], F32R)
        ident = sb("ident", [128, 128])
        vec = sb("vec", [128, N_VEC])
        rows = sb("rows", [128, 8])
        der = sb("der", [128, 13])
        bmsg = sb("bmsg", [128, T, 128])
        half_pow = sb("half_pow", [128, T])
        neg_half_pow = sb("neg_half_pow", [128, T])
        art = sb("art", [128, (B + 1) * T])
        x_rows = [sb(f"x_rows{i}", [128, T, 128]) for i in range(2)]
        xt = sb("xt", [128, T, 128])
        xt_hi = sb("xt_hi", [128, T, 128], F32R)
        xt_lo = sb("xt_lo", [128, T, 128], F32R)
        supp = sb("supp", [128, N])
        supp_sq = sb("supp_sq", [128, T, 128])
        ss = sb("ss", [128, T])
        norm0 = sb("norm0", [128, T])
        norm = sb("norm", [128, T])
        rnorm = sb("rnorm", [128, T])
        th = sb("th", [128, T])
        fac = sb("fac", [128, T])
        y1 = sb("y1", [128, T, 128])
        st1 = sb("st1", [128, T, 6])
        mv1 = sb("mv1", [128, 3, T])
        ve1 = sb("ve1", [128, T])
        rstd1 = sb("rstd1", [128, T])
        x1_rows = [sb(f"x1_rows{i}", [128, T, 128]) for i in range(2)]
        x1t = [sb(f"x1t{i}", [128, N]) for i in range(2)]
        x1t_hi = [sb(f"x1t_hi{i}", [128, N], F32R) for i in range(2)]
        x1t_lo = [sb(f"x1t_lo{i}", [128, N], F32R) for i in range(2)]
        h = sb("h", [128, 3, HW])
        h_hi = sb("h_hi", [128, 3, HW], F32R)
        h_lo = sb("h_lo", [128, 3, HW], F32R)
        x1_bias = sb("x1_bias", [128, N])

        prep = ExitStack()
        CH = 4
        NB = B * T // CH
        x_all = [sb(f"x_all{c}", [128, NB, 128], where=prep) for c in range(CH)]
        w2_st = sb("w2_st", [128, TAPS, 128], where=prep)
        filt = sb("filt", [128, 2, HT, 128], where=prep)
        gru_st = sb("gru_st", [128, 9, 128], where=prep)
        small_st = sb("small_st", [128, 3, 128], where=prep)
        sm = [sb(f"sm{i}", [128, B * T], where=prep) for i in range(8)]
        prep.close()

        e = sb("e", [128, T, N])
        am_hi = sb("am_hi", [128, T, N], F32R)
        am_lo = sb("am_lo", [128, T, N], F32R)
        msg = sb("msg", [128, T, 128])
        msg_hi = sb("msg_hi", [128, T, 128], F32R)
        msg_lo = sb("msg_lo", [128, T, 128], F32R)
        s_mix = sb("s_mix", [128, N])
        q = sb("q", [128, N])
        q_hi = sb("q_hi", [128, N], F32R)
        ta = sb("ta", [128, N])
        tb = sb("tb", [128, N])
        da = sb("da", [128, N], F32R)
        db = sb("db", [128, N], F32R)
        cz = sb("cz", [128, N])
        cv = sb("cv", [128, N])
        xc_hi = sb("xc_hi", [128, N], F32R)
        xc_lo = sb("xc_lo", [128, N], F32R)
        nm_hi = sb("nm_hi", [128, N], F32R)
        nm_lo = sb("nm_lo", [128, N], F32R)
        tr = sb("tr", [128, N])
        tz = sb("tz", [128, N])
        ghn = sb("ghn", [128, N])
        un = sb("un", [128, N])
        nn = sb("nn", [128, N])
        xd = sb("xd", [128, N])
        o = sb("o", [128, N])
        y2 = sb("y2", [128, T, 128])
        st2 = sb("st2", [128, T, 6])
        mv2 = sb("mv2", [128, 3, T])
        ve2 = sb("ve2", [128, T])
        rstd2 = sb("rstd2", [128, T])
        y_out = [sb(f"y_out{i}", [128, T, 128]) for i in range(2)]

        names = """prep_x0 prep_x1 prep_x2 prep_x3 prep_w2 prep_gru prep_small prep_vec adj_in0 adj_in1
            x_in0 x_in1 stored0 stored1
            sq_done ssum_done small_step root_done ln_done ln_ready art_done pool_const pad_done
            vec_step vec_eps vec_pow vec_done filt_done wsplit_hi wsplit_lo
            xt_done xt_hi_done xt_lo_done adj_hi_done adj_lo_done pow_ns pow_v1 pow_v2 xd_done
            conv1_done se_done msg_mm ghn_mm conv_p1 conv2_done dist_mm supp_mm srow_mm out_mm nmp_mm
            r_mm z_mm n_mm x1t_mm
            tr_done tz_done h_done smix_done nn_done msg_hi_done ghn_done tatb_done exp_done
            supp_out ss_done th_done xc_hi_done nm_hi_done x1t_out
            un_done npre_done hhi_done hlo_done hsum_done shi_done slo_done q_done qhi_done da_done dadb_done
            msgv_done msglo_done gate_done o_done am_done amhi_done amlo_done norm_done rnorm_done fac_done
            y1_done st1_done mv1_done ve1_done x1_done cz_done cv_done xc_lo_done
            y2_done st2_done mv2_done ve2_done out_done nm_lo_done x1t_lo_done""".split()
        S = {n: sem(n) for n in names}

        def at(b, per, k):
            return b * per + k

        xr_dram = x.rearrange("b (t p) d -> b p t d", p=128)
        adj_dram = adj_t.rearrange("b (t p) i -> b p t i", p=128)
        out_dram = out.rearrange("b (t p) d -> b p t d", p=128)

        def row_of(dram, b):
            return dram[b] if isinstance(b, int) else dram[bass.ds(b, 1)].rearrange("a p t d -> (a p) t d")

        def cast_r(ap):
            return ap

        block = ctx.enter_context(nc.Block())

        @block.sync
        def _(sp):
            def load_x(b, par, turn):
                sp.dma_start(x_rows[par][:], row_of(xr_dram, b)).then_inc(S[f"x_in{par}"], 16)

            def load_adj(b, par, turn):
                sp.dma_start(adj_sb[par][:], row_of(adj_dram, b)).then_inc(S[f"adj_in{par}"], 16)

            def load(n, par):
                sp.wait_ge(S["y1_done"], at(n - 2, T, T))
                load_x(n, par, None)
                sp.wait_ge(S["am_done"], at(n - 2, T, T))
                sp.wait_ge(S["adj_lo_done"], at(n - 2, T, T))
                load_adj(n, par, None)

            def store(b, par):
                sp.wait_ge(S["out_done"], at(b, T, T))
                sp.dma_start(row_of(out_dram, b), y_out[par][:]).then_inc(S[f"stored{par}"], 16)

            x_chunks = x.rearrange("(c b) (t p) d -> c p (b t) d", c=CH, p=128)
            sp.dma_start(vec[:], vectors).then_inc(S["prep_vec"], 16)
            sp.dma_start(rows[:], rows_const).then_inc(S["prep_vec"], 16)
            for c in range(CH):
                sp.dma_start(x_all[c][:], x_chunks[c]).then_inc(S[f"prep_x{c}"], 16)
                if c == 0:
                    sp.dma_start(small_st[:], w_small).then_inc(S["prep_small"], 16)
                    sp.dma_start(w2_st[:], w_conv2).then_inc(S["prep_w2"], 16)
            sp.dma_start(ident[:], ident_in).then_inc(S["prep_vec"], 16)
            sp.dma_start(bmsg[:], b_msg.rearrange("(a c d) -> a c d", a=1, c=1).to_broadcast([128, T, 128])
                         ).then_inc(S["prep_vec"], 16)
            load_x(0, 0, None)
            load_adj(0, 0, None)
            sp.dma_start(gru_st[:], w_gru).then_inc(S["prep_gru"], 16)
            load_x(1, 1, None)
            load_adj(1, 1, None)
            load(2, 0)
            with sp.Fori(3, B - 1, 2) as n:
                load(n, 1)
                store(n - 3, 0)
                load(n + 1, 0)
                store(n - 2, 1)
            load(B - 1, 1)
            for b in range(B - 4, B):
                store(b, b % 2)
            for par in range(2):
                sp.wait_ge(S[f"stored{par}"], 16 * (B // 2))

        @block.gpsimd
        def _(pool):
            pool.memset(half_pow[:], 0.5).then_inc(S["pool_const"], 1)
            pool.memset(neg_half_pow[:], -0.5).then_inc(S["pool_const"], 1)
            pool.wait_ge(S["pool_const"], 2)
            pool.wait_ge(S["vec_eps"], 2)
            pool.tensor_tensor(der[:, W_T3:W_T3 + 2], der[:, W_T1:W_T1 + 2], neg_half_pow[:, 0:2], ALU.pow
                               ).then_inc(S["vec_pow"], 1)

            def xt_split(n, par, turn):
                pool.wait_ge(S[f"x_in{par}"], turn)
                if isinstance(n, int) and n == 0:
                    pool.wait_ge(S["art_done"], 1)
                else:
                    pool.wait_ge(S["supp_mm"], n)
                a = art[:, n * T:(n + 1) * T] if isinstance(n, int) else art[:, bass.ds(n * T, T)]
                a_all = a.unsqueeze(2).to_broadcast([128, T, 128])
                pool.tensor_tensor(xt[:], x_rows[par][:], a_all, ALU.mult).then_inc(S["xt_done"], 1)
                pool.tensor_tensor(xt_hi[:], x_rows[par][:], a_all, ALU.mult).then_inc(S["xt_hi_done"], 1)
                pool.wait_ge(S["xt_done"], n + 1)
                pool.wait_ge(S["xt_hi_done"], n + 1)
                pool.tensor_tensor(xt_lo[:], xt[:], xt_hi[:].bitcast(F32), ALU.subtract).then_inc(S["xt_lo_done"], 1)

            def adj_low(n, par):
                for t in range(T):
                    pool.wait_ge(S["adj_hi_done"], at(n, T, t + 1))
                    pool.tensor_tensor(adj_lo[:, t, :], adj_sb[par][:, t, :], adj_hi[:, t, :].bitcast(F32),
                                       ALU.subtract).then_inc(S["adj_lo_done"], 1)

            def front_pows(n):
                pool.wait_ge(S["ss_done"], at(n, T, T))
                pool.tensor_tensor(norm0[:], ss[:], half_pow[:], ALU.pow).then_inc(S["pow_ns"], 1)
                pool.wait_ge(S["ve1_done"], n + 1)
                pool.tensor_tensor(rstd1[:], ve1[:], neg_half_pow[:], ALU.pow).then_inc(S["pow_v1"], 1)

            def tail_xd(t, par):
                pool.wait_ge(S["nn_done"], t + 1)
                pool.tensor_tensor(xd[:], x1t[par][:], nn[:], ALU.subtract).then_inc(S["xd_done"], 1)

            def tail_pow(t):
                pool.wait_ge(S["ve2_done"], t + 1)
                pool.tensor_tensor(rstd2[:], ve2[:], neg_half_pow[:], ALU.pow).then_inc(S["pow_v2"], 1)

            def step(b, par, first=False, last=False, in_turn=None):
                n, t = b + 1, b - 1
                if not last:
                    xt_split(n, 1 - par, in_turn)
                if not first:
                    tail_xd(t, 1 - par)
                if not last:
                    adj_low(n, 1 - par)
                    front_pows(n)
                if not first:
                    tail_pow(t)

            xt_split(0, 0, 16)
            adj_low(0, 0)
            front_pows(0)
            step(0, 0, first=True, in_turn=16)
            with pool.Fori(1, B - 1, 2) as b:
                step(b, 1, in_turn=8 * b + 24)
                step(b + 1, 0, in_turn=8 * b + 24)
            step(B - 1, 1, last=True)
            tail_xd(B - 1, 1)
            tail_pow(B - 1)

        @block.scalar
        def _(act):
            for c in range(CH):
                act.wait_ge(S[f"prep_x{c}"], 16)
                act.activation(x_all[c][:], x_all[c][:], ACT.Square).then_inc(S["sq_done"], 1)
            act.wait_ge(S["ssum_done"], CH + 1)
            act.activation(sm[1][:], sm[0][:], ACT.Sqrt).then_inc(S["root_done"], 1)
            act.wait_ge(S["ln_ready"], 1)
            act.activation(sm[5][:], sm[4][:], ACT.Ln).then_inc(S["ln_done"], 1)

            def adj_high(n, par, turn):
                act.wait_ge(S[f"adj_in{par}"], turn)
                if not (isinstance(n, int) and n == 0):
                    act.wait_ge(S["supp_mm"], n)
                for t in range(T):
                    act.activation(adj_hi[:, t, :], adj_sb[par][:, t, :], ACT.Copy).then_inc(S["adj_hi_done"], 1)

            def front_support(n):
                act.wait_ge(S["supp_mm"], n + 1)
                act.activation(supp[:], bank_y[:], ACT.Copy).then_inc(S["supp_out"], 1)

            def front_squares(n):
                act.wait_ge(S["srow_mm"], n + 1)
                for t in range(T):
                    act.activation(supp_sq[:, t, :], bank_x[:, t * 128:(t + 1) * 128], ACT.Square,
                                   accum_out=ss[:, t:t + 1]).then_inc(S["ss_done"], 1)

            def front_tanh(n):
                act.wait_ge(S["norm_done"], n + 1)
                act.activation(th[:], norm[:], ACT.Tanh).then_inc(S["th_done"], 1)

            def front_x1t(n, par):
                act.wait_ge(S["x1t_mm"], n + 1)
                act.activation(x1t_hi[par][:], bank_x[:], ACT.Copy)
                act.activation(x1t[par][:], bank_x[:], ACT.Copy).then_inc(S["x1t_out"], 1)
                act.activation(x1_bias[:], bank_x[:], ACT.Identity, bias=der[:, W_BI2:W_BI2 + 1]
                               ).then_inc(S["x1t_out"], 1)

            def tail_rz(t):
                act.wait_ge(S["r_mm"], t + 1)
                act.activation(tr[:], bank_a[0][:], ACT.Tanh, bias=der[:, W_HR:W_HR + 1], scale=0.5
                               ).then_inc(S["tr_done"], 1)
                act.wait_ge(S["z_mm"], t + 1)
                act.activation(tz[:], bank_a[1][:], ACT.Tanh, bias=der[:, W_HZ:W_HZ + 1], scale=0.5
                               ).then_inc(S["tz_done"], 1)

            def tail_n(t):
                act.wait_ge(S["npre_done"], t + 1)
                act.activation(nn[:], un[:], ACT.Tanh, bias=vec[:, V_IN:V_IN + 1]).then_inc(S["nn_done"], 1)

            def main_h(b):
                act.wait_ge(S["conv1_done"], b + 1)
                act.activation(h[:, 0:2, PAD // 2:PAD // 2 + HALF], bank_x[:].rearrange("p (m g) -> p g m", g=2),
                               ACT.Relu, bias=der[:, W_BI1:W_BI1 + 1], scale=der[:, W_SC1:W_SC1 + 1]
                               ).then_inc(S["h_done"], 1)

            def main_mix(b):
                act.wait_ge(S["se_done"], b + 1)
                act.activation(s_mix[:], bank_y[:], ACT.Identity, bias=der[:, W_NU:W_NU + 1],
                               scale=rows[:, C_MU:C_MU + 1]).then_inc(S["smix_done"], 1)

            def main_ghn(b):
                act.wait_ge(S["ghn_mm"], b + 1)
                act.activation(ghn[:], bank_v[:], ACT.Identity, bias=der[:, W_HHN:W_HHN + 1], scale=0.5
                               ).then_inc(S["ghn_done"], 1)

            def main_msg(b):
                act.wait_ge(S["msgv_done"], b + 1)
                act.activation(msg_hi[:], msg[:], ACT.Relu).then_inc(S["msg_hi_done"], 1)

            def main_tab(b):
                act.wait_ge(S["q_done"], b + 1)
                act.activation(ta[:], q[:], ACT.Identity, bias=rows[:, C_BA:C_BA + 1], scale=rows[:, C_AA:C_AA + 1]
                               ).then_inc(S["tatb_done"], 1)
                act.activation(tb[:], q[:], ACT.Identity, bias=rows[:, C_BB:C_BB + 1], scale=rows[:, C_AB:C_AB + 1]
                               ).then_inc(S["tatb_done"], 1)

            def main_exp(b, t):
                act.wait_ge(S["dist_mm"], at(b, T, t + 1))
                act.activation(e[:, t, :], bank_a[t % 2][:], ACT.Exp, scale=2.0).then_inc(S["exp_done"], 1)

            def main_amhi(b, t):
                act.wait_ge(S["am_done"], at(b, T, t + 1))
                act.activation(am_hi[:, t, :], e[:, t, :], ACT.Copy).then_inc(S["amhi_done"], 1)

            def main_conv_hi(b):
                act.wait_ge(S["cv_done"], b + 1)
                act.activation(xc_hi[:], cv[:], ACT.Relu).then_inc(S["xc_hi_done"], 1)

            def main_nm_hi(b):
                act.wait_ge(S["nmp_mm"], b + 1)
                act.activation(nm_hi[:], bank_y[:], ACT.Copy).then_inc(S["nm_hi_done"], 1)

            def step(b, par, first=False, last=False, in_turn=None):
                n, t = b + 1, b - 1
                if not first:
                    tail_rz(t)
                main_h(b)
                main_mix(b)
                if not last:
                    adj_high(n, 1 - par, in_turn)
                if not first:
                    tail_n(t)
                main_tab(b)
                main_msg(b)
                main_ghn(b)
                main_exp(b, 0)
                main_exp(b, 1)
                if not last:
                    front_support(n)
                main_exp(b, 2)
                main_exp(b, 3)
                if not last:
                    front_squares(n)
                for k in range(T):
                    main_amhi(b, k)
                if not last:
                    front_tanh(n)
                main_conv_hi(b)
                main_nm_hi(b)
                if not last:
                    front_x1t(n, 1 - par)

            adj_high(0, 0, 16)
            act.wait_ge(S["vec_done"], 1)
            front_support(0)
            front_squares(0)
            front_tanh(0)
            front_x1t(0, 0)
            step(0, 0, first=True, in_turn=16)
            with act.Fori(1, B - 1, 2) as b:
                step(b, 1, in_turn=8 * b + 24)
                step(b + 1, 0, in_turn=8 * b + 24)
            step(B - 1, 1, last=True)
            tail_rz(B - 1)
            tail_n(B - 1)

        @block.vector
        def _(dve):
            steps = [0]

            def small(ins):
                steps[0] += 1
                ins.then_inc(S["small_step"], 1)
                dve.wait_ge(S["small_step"], steps[0])

            for buf in (h, h_hi, h_lo):
                v = buf[:] if buf is h else buf[:].bitcast(F32)
                dve.memset(v[:, :, 0:PAD // 2], 0.0)
                dve.memset(v[:, :, PAD // 2 + HALF:HW], 0.0).then_inc(S["pad_done"], 1)

            dve.wait_ge(S["prep_vec"], 64)
            dve.tensor_scalar(der[:, W_T1:W_T1 + 1], vec[:, V_V1:V_V1 + 1], EPS, None, ALU.add).then_inc(S["vec_eps"], 1)
            dve.tensor_scalar(der[:, W_T2:W_T2 + 1], vec[:, V_V2:V_V2 + 1], EPS, None, ALU.add).then_inc(S["vec_eps"], 1)
            small(dve.tensor_tensor(der[:, W_HR:W_HR + 2], vec[:, V_IR:V_IR + 2], vec[:, V_HR:V_HR + 2], ALU.add))
            small(dve.tensor_scalar(der[:, W_HR:W_HR + 2], der[:, W_HR:W_HR + 2], 0.5, None, ALU.mult))
            small(dve.tensor_scalar(der[:, W_HHN:W_HHN + 1], vec[:, V_HN:V_HN + 1], 0.5, None, ALU.mult))
            small(dve.tensor_tensor(der[:, W_NU:W_NU + 1], vec[:, V_SE:V_SE + 1], rows[:, C_MU:C_MU + 1], ALU.mult))
            small(dve.tensor_tensor(der[:, W_NU:W_NU + 1], der[:, W_NU:W_NU + 1], rows[:, C_NU:C_NU + 1], ALU.add))
            dve.wait_ge(S["vec_pow"], 1)
            for k, (g, bb, m, sc, bi) in enumerate(((V_G1, V_B1, V_M1, W_SC1, W_BI1), (V_G2, V_B2, V_M2, W_SC2, W_BI2))):
                small(dve.tensor_tensor(der[:, sc:sc + 1], vec[:, g:g + 1], der[:, W_T3 + k:W_T3 + k + 1], ALU.mult))
                small(dve.tensor_tensor(der[:, bi:bi + 1], vec[:, m:m + 1], der[:, sc:sc + 1], ALU.mult))
                small(dve.tensor_tensor(der[:, bi:bi + 1], vec[:, bb:bb + 1], der[:, bi:bi + 1], ALU.subtract))
            dve.engine_nop().then_inc(S["vec_done"], 1) if False else dve.tensor_copy(
                der[:, W_N:W_N + 1], vec[:, V_IN:V_IN + 1]).then_inc(S["vec_done"], 1)

            def sums(c):
                dve.wait_ge(S["sq_done"], c + 1)
                dve.tensor_reduce(sm[0][:, c * NB:(c + 1) * NB], x_all[c][:], AX.X, ALU.add).then_inc(S["ssum_done"], 1)

            sums(0)
            dve.wait_ge(S["prep_small"], 16)
            small(dve.tensor_copy(small_hi[:], small_st[:]))
            dve.tensor_tensor(small_lo[:], small_st[:], small_hi[:].bitcast(F32), ALU.subtract).then_inc(S["wsplit_lo"], 1)
            sums(1)
            dve.wait_ge(S["prep_w2"], 16)
            even = w2_st[:, 0:TAPS:2, :]
            odd = w2_st[:, 1:TAPS:2, :]
            dve.tensor_tensor(filt[:, 0, 0:HT - 1, :], odd, even[:, 0:HT - 1, :], ALU.subtract)
            dve.tensor_scalar(filt[:, 0, HT - 1, :], even[:, HT - 1, :], -1.0, None, ALU.mult)
            dve.tensor_tensor(filt[:, 1, 1:HT, :], odd, even[:, 1:HT, :], ALU.subtract)
            small(dve.tensor_scalar(filt[:, 1, 0, :], even[:, 0, :], -1.0, None, ALU.mult))
            dve.tensor_copy(conv_hi[:, 0, :, :], even)
            small(dve.tensor_copy(conv_hi[:, 1:3, :, :], filt[:]))
            sums(2)
            dve.tensor_tensor(conv_lo[:, 0, :, :], even, conv_hi[:, 0, :, :].bitcast(F32), ALU.subtract)
            dve.tensor_tensor(conv_lo[:, 1:3, :, :], filt[:], conv_hi[:, 1:3, :, :].bitcast(F32), ALU.subtract
                              ).then_inc(S["wsplit_lo"], 1)
            sums(3)
            dve.wait_ge(S["ssum_done"], CH)
            dve.tensor_scalar(sm[0][:], sm[0][:], MIN_NORM * MIN_NORM, None, ALU.max).then_inc(S["ssum_done"], 1)
            dve.wait_ge(S["root_done"], 1)
            small(dve.reciprocal(sm[2][:], sm[1][:]))
            small(dve.tensor_tensor(sm[2][:], sm[0][:], sm[2][:], ALU.mult))
            small(dve.tensor_tensor(sm[2][:], sm[1][:], sm[2][:], ALU.add))
            small(dve.tensor_scalar(sm[2][:], sm[2][:], 0.5, MIN_NORM, ALU.mult, ALU.max))
            small(dve.tensor_scalar(sm[3][:], sm[2][:], ARTANH_MAX, None, ALU.min))
            small(dve.tensor_scalar(sm[6][:], sm[3][:], -1.0, 1.0, ALU.mult, ALU.add))
            small(dve.reciprocal(sm[6][:], sm[6][:]))
            small(dve.scalar_tensor_tensor(sm[4][:], sm[3][:], 1.0, sm[6][:], ALU.add, ALU.mult))
            dve.tensor_scalar(sm[7][:], sm[3][:], SERIES_BELOW, None, ALU.is_lt).then_inc(S["ln_ready"], 1)
            small(dve.tensor_tensor(sm[3][:], sm[3][:], sm[3][:], ALU.mult))
            small(dve.tensor_scalar(sm[6][:], sm[3][:], SERIES[-1], None, ALU.mult))
            for c in SERIES[-2:0:-1]:
                small(dve.scalar_tensor_tensor(sm[6][:], sm[6][:], c, sm[3][:], ALU.add, ALU.mult))
            small(dve.tensor_scalar(sm[6][:], sm[6][:], SERIES[0], None, ALU.add))
            small(dve.reciprocal(sm[2][:], sm[2][:]))
            dve.wait_ge(S["ln_done"], 1)
            small(dve.scalar_tensor_tensor(sm[5][:], sm[5][:], 0.5, sm[2][:], ALU.mult, ALU.mult))
            small(dve.tensor_tensor(sm[6][:], sm[6][:], sm[5][:], ALU.subtract))
            small(dve.tensor_tensor(sm[6][:], sm[6][:], sm[7][:], ALU.mult))
            dve.tensor_tensor(art[:, 0:B * T], sm[5][:], sm[6][:], ALU.add).then_inc(S["art_done"], 1)

            dve.wait_ge(S["prep_gru"], 16)
            small(dve.tensor_copy(gru_hi[:], gru_st[:]))
            dve.tensor_tensor(gru_lo[:], gru_st[:], gru_hi[:].bitcast(F32), ALU.subtract).then_inc(S["wsplit_lo"], 1)

            def front_factor(n):
                dve.wait_ge(S["pow_ns"], n + 1)
                dve.tensor_scalar(norm[:], norm0[:], MIN_NORM, None, ALU.max).then_inc(S["norm_done"], 1)
                dve.wait_ge(S["norm_done"], n + 1)
                dve.reciprocal(rnorm[:], norm[:]).then_inc(S["rnorm_done"], 1)
                dve.wait_ge(S["rnorm_done"], n + 1)
                dve.wait_ge(S["th_done"], n + 1)
                dve.scalar_tensor_tensor(fac[:], th[:], MAX_NORM, rnorm[:], ALU.min, ALU.mult).then_inc(S["fac_done"], 1)

            def front_y1(n, par):
                dve.wait_ge(S["fac_done"], n + 1)
                for t in range(T):
                    dve.scalar_tensor_tensor(y1[:, t, :], bank_x[:, t * 128:(t + 1) * 128], fac[:, t:t + 1],
                                             x_rows[par][:, t, :], ALU.mult, ALU.add).then_inc(S["y1_done"], 1)

            def stats(y, st, mv, ve, b, y_sem, y_per, st_sem, mv_sem, ve_sem):
                for t in range(T):
                    dve.wait_ge(S[y_sem], at(b, y_per, min(t + 1, y_per)))
                    dve.bn_stats(st[:, t, :], y[:, t, :]).then_inc(S[st_sem], 1)
                dve.wait_ge(S[st_sem], at(b, T, T))
                dve.tensor_tensor(mv[:, 0, :], st[:, :, 1], st[:, :, 4], ALU.add)
                dve.tensor_tensor(mv[:, 1, :], st[:, :, 1], st[:, :, 4], ALU.subtract)
                dve.tensor_tensor(mv[:, 2, :], st[:, :, 2], st[:, :, 5], ALU.add).then_inc(S[mv_sem], 1)
                dve.wait_ge(S[mv_sem], at(b, 2, 1))
                dve.tensor_scalar(mv[:, 0, :], mv[:, 0, :], 0.5, None, ALU.mult)
                dve.scalar_tensor_tensor(mv[:, 1, :], mv[:, 1, :], 0.25, mv[:, 1, :], ALU.mult, ALU.mult)
                dve.tensor_scalar(mv[:, 2, :], mv[:, 2, :], 1.0 / D, EPS, ALU.mult, ALU.add).then_inc(S[mv_sem], 1)
                dve.wait_ge(S[mv_sem], at(b, 2, 2))
                dve.tensor_tensor(ve[:], mv[:, 1, :], mv[:, 2, :], ALU.add).then_inc(S[ve_sem], 1)

            def front_x1(n, par):
                if not (isinstance(n, int) and n < 2):
                    dve.wait_ge(S["y2_done"], n - 1)
                dve.wait_ge(S["pow_v1"], n + 1)
                for t in range(T):
                    dve.tensor_scalar(x1_rows[par][:, t, :], y1[:, t, :], mv1[:, 0, t:t + 1], rstd1[:, t:t + 1],
                                      ALU.subtract, ALU.mult).then_inc(S["x1_done"], 1)

            def front_x1lo(n, par):
                dve.wait_ge(S["x1t_out"], at(n, 2, 1))
                dve.tensor_tensor(x1t_lo[par][:], x1t[par][:], x1t_hi[par][:].bitcast(F32), ALU.subtract
                                  ).then_inc(S["x1t_lo_done"], 1)

            def tail_un(t):
                dve.wait_ge(S["tr_done"], t + 1)
                dve.wait_ge(S["ghn_done"], t + 1)
                dve.scalar_tensor_tensor(un[:], tr[:], 1.0, ghn[:], ALU.add, ALU.mult).then_inc(S["un_done"], 1)
                dve.wait_ge(S["un_done"], t + 1)
                dve.wait_ge(S["n_mm"], t + 1)
                dve.tensor_tensor(un[:], bank_p[:], un[:], ALU.add).then_inc(S["npre_done"], 1)

            def tail_o(t):
                dve.wait_ge(S["xd_done"], t + 1)
                dve.wait_ge(S["tz_done"], t + 1)
                dve.scalar_tensor_tensor(xd[:], tz[:], 1.0, xd[:], ALU.add, ALU.mult).then_inc(S["gate_done"], 1)
                dve.wait_ge(S["gate_done"], t + 1)
                dve.scalar_tensor_tensor(o[:], xd[:], 0.5, nn[:], ALU.mult, ALU.add).then_inc(S["o_done"], 1)

            def tail_y2(t, par):
                dve.wait_ge(S["out_mm"], t + 1)
                dve.tensor_tensor(y2[:], bank_w[:].rearrange("p (t d) -> p t d", t=T), x1_rows[par][:], ALU.add
                                  ).then_inc(S["y2_done"], 1)

            def tail_stats(t):
                stats(y2, st2, mv2, ve2, t, "y2_done", 1, "st2_done", "mv2_done", "ve2_done")

            def tail_out(t, par, stored):
                dve.wait_ge(S["pow_v2"], t + 1)
                if stored is not None:
                    dve.wait_ge(S[f"stored{par}"], stored)
                for k in range(T):
                    dve.tensor_scalar(y_out[par][:, k, :], y2[:, k, :], mv2[:, 0, k:k + 1], rstd2[:, k:k + 1],
                                      ALU.subtract, ALU.mult).then_inc(S["out_done"], 1)

            def main_h(b):
                dve.wait_ge(S["h_done"], b + 1)
                dve.tensor_copy(h_hi[:, 0:2, :], h[:, 0:2, :]).then_inc(S["hhi_done"], 1)
                dve.wait_ge(S["hhi_done"], b + 1)
                dve.tensor_tensor(h_lo[:, 0:2, :], h[:, 0:2, :], h_hi[:, 0:2, :].bitcast(F32), ALU.subtract
                                  ).then_inc(S["hlo_done"], 1)
                dve.tensor_tensor(h[:, 2, :], h[:, 0, :], h[:, 1, :], ALU.add).then_inc(S["hsum_done"], 1)
                dve.wait_ge(S["hsum_done"], b + 1)
                dve.tensor_copy(h_hi[:, 2, :], h[:, 2, :]).then_inc(S["shi_done"], 1)
                dve.wait_ge(S["shi_done"], b + 1)
                dve.tensor_tensor(h_lo[:, 2, :], h[:, 2, :], h_hi[:, 2, :].bitcast(F32), ALU.subtract
                                  ).then_inc(S["slo_done"], 1)

            def main_q(b):
                dve.wait_ge(S["smix_done"], b + 1)
                dve.scalar_tensor_tensor(q[:], bank_y[:], vec[:, V_SE:V_SE + 1], s_mix[:], ALU.add, ALU.mult
                                         ).then_inc(S["q_done"], 1)
                dve.wait_ge(S["q_done"], b + 1)
                dve.tensor_copy(q_hi[:], q[:]).then_inc(S["qhi_done"], 1)

            def main_dab(b):
                dve.wait_ge(S["qhi_done"], b + 1)
                dve.wait_ge(S["tatb_done"], at(b, 2, 2))
                dve.scalar_tensor_tensor(da[:], q_hi[:].bitcast(F32), rows[:, C_CA:C_CA + 1], ta[:], ALU.mult, ALU.add
                                         ).then_inc(S["da_done"], 1)
                dve.scalar_tensor_tensor(db[:], q_hi[:].bitcast(F32), rows[:, C_CB:C_CB + 1], tb[:], ALU.mult, ALU.add
                                         ).then_inc(S["dadb_done"], 1)

            def main_msgv(b):
                dve.wait_ge(S["msg_mm"], b + 1)
                dve.tensor_tensor(msg[:], bank_w[:].rearrange("p (t d) -> p t d", t=T), bmsg[:], ALU.add
                                  ).then_inc(S["msgv_done"], 1)

            def main_msglo(b):
                dve.wait_ge(S["msg_hi_done"], b + 1)
                dve.scalar_tensor_tensor(msg_lo[:], msg[:], 0.0, msg_hi[:].bitcast(F32), ALU.max, ALU.subtract
                                         ).then_inc(S["msglo_done"], 1)

            def main_am(b, par, t):
                dve.wait_ge(S["exp_done"], at(b, T, t + 1))
                dve.tensor_tensor(e[:, t, :], e[:, t, :], adj_sb[par][:, t, :], ALU.mult).then_inc(S["am_done"], 1)

            def main_amlo(b, t):
                dve.wait_ge(S["amhi_done"], at(b, T, t + 1))
                dve.tensor_tensor(am_lo[:, t, :], e[:, t, :], am_hi[:, t, :].bitcast(F32), ALU.subtract
                                  ).then_inc(S["amlo_done"], 1)

            def main_conv(b):
                dve.wait_ge(S["conv2_done"], b + 1)
                dve.wait_ge(S["x1t_out"], at(b, 2, 2))
                xb = x1_bias[:].rearrange("p (m g) -> p g m", g=2)
                zv = cz[:].rearrange("p (g m) -> p g m", g=2)
                for g in range(2):
                    ins = dve.scalar_tensor_tensor(zv[:, g, :], bank_p[:, 0:HALF], der[:, W_SC2:W_SC2 + 1],
                                                   xb[:, g, :], ALU.mult, ALU.add)
                ins.then_inc(S["cz_done"], 1)
                dve.wait_ge(S["cz_done"], b + 1)
                dve.scalar_tensor_tensor(cv[:].rearrange("p (m g) -> p g m", g=2),
                                         bank_c[:].rearrange("p (g m) -> p g m", g=2), der[:, W_SC2:W_SC2 + 1],
                                         zv, ALU.mult, ALU.add).then_inc(S["cv_done"], 1)

            def main_conv_lo(b):
                dve.wait_ge(S["xc_hi_done"], b + 1)
                dve.scalar_tensor_tensor(xc_lo[:], cv[:], 0.0, xc_hi[:].bitcast(F32), ALU.max, ALU.subtract
                                         ).then_inc(S["xc_lo_done"], 1)

            def main_nm_lo(b):
                dve.wait_ge(S["nm_hi_done"], b + 1)
                dve.tensor_tensor(nm_lo[:], bank_y[:], nm_hi[:].bitcast(F32), ALU.subtract).then_inc(S["nm_lo_done"], 1)

            def step(b, par, first=False, last=False, stored=None):
                n, t = b + 1, b - 1
                if not first:
                    tail_un(t)
                main_h(b)
                main_q(b)
                main_msgv(b)
                main_dab(b)
                if not first:
                    tail_o(t)
                main_msglo(b)
                for k in (0, 1):
                    main_am(b, par, k)
                for k in (0, 1):
                    main_amlo(b, k)
                for k in (2, 3):
                    main_am(b, par, k)
                for k in (2, 3):
                    main_amlo(b, k)
                if not last:
                    front_factor(n)
                    front_y1(n, 1 - par)
                    stats(y1, st1, mv1, ve1, n, "y1_done", T, "st1_done", "mv1_done", "ve1_done")
                main_conv(b)
                if not first:
                    tail_y2(t, 1 - par)
                if not last:
                    front_x1(n, 1 - par)
                main_conv_lo(b)
                if not first:
                    tail_stats(t)
                main_nm_lo(b)
                if not last:
                    front_x1lo(n, 1 - par)
                if not first:
                    tail_out(t, 1 - par, stored)

            front_factor(0)
            front_y1(0, 0)
            stats(y1, st1, mv1, ve1, 0, "y1_done", T, "st1_done", "mv1_done", "ve1_done")
            front_x1(0, 0)
            front_x1lo(0, 0)
            step(0, 0, first=True)
            step(1, 1)
            step(2, 0)
            with dve.Fori(3, B - 1, 2) as b:
                step(b, 1, stored=8 * b - 8)
                step(b + 1, 0, stored=8 * b - 8)
            step(B - 1, 1, last=True, stored=16 * ((B - 4) // 2 + 1))
            tail_un(B - 1)
            tail_o(B - 1)
            tail_y2(B - 1, 1)
            tail_stats(B - 1)
            tail_out(B - 1, 1, 16 * ((B - 3) // 2 + 1))

        @block.tensor
        def _(pe):
            def passes(out_ap, w_hi, w_lo, v_hi, v_lo, start=True, stop=True):
                pe.matmul(out_ap, w_hi, v_hi, start=start, stop=False)
                pe.matmul(out_ap, w_lo, v_hi, start=False, stop=False)
                return pe.matmul(out_ap, w_hi, v_lo, start=False, stop=stop)

            def front_support(n):
                pe.wait_ge(S["xt_lo_done"], n + 1)
                for t in range(T):
                    pe.wait_ge(S["adj_lo_done"], at(n, T, t + 1))
                    last = passes(bank_y[:], xt_hi[:, t, :], xt_lo[:, t, :], adj_hi[:, t, :], adj_lo[:, t, :],
                                  start=t == 0, stop=t == T - 1)
                last.then_inc(S["supp_mm"], 1)

            def front_rows(n):
                pe.wait_ge(S["supp_out"], n + 1)
                for t in range(T):
                    last = pe.transpose(bank_x[:, t * 128:(t + 1) * 128], supp[:, t * 128:(t + 1) * 128], ident[:])
                last.then_inc(S["srow_mm"], 1)

            def front_x1t(n, par):
                for t in range(T):
                    pe.wait_ge(S["x1_done"], at(n, T, t + 1))
                    last = pe.transpose(bank_x[:, t * 128:(t + 1) * 128], x1_rows[par][:, t, :], ident[:])
                last.then_inc(S["x1t_mm"], 1)

            def tail_rows(t):
                pe.wait_ge(S["o_done"], t + 1)
                for k in range(T):
                    last = pe.transpose(bank_w[:, k * 128:(k + 1) * 128], o[:, k * 128:(k + 1) * 128], ident[:])
                last.then_inc(S["out_mm"], 1)

            def conv_part(b, p, which):
                out_ap = (bank_p[:, 0:HALF], bank_c[:, 0:HALF], bank_c[:, HALF:N])[p]
                sig = (2, 1, 0)[p]
                w = conv_lo if which == 1 else conv_hi
                v = h_lo if which == 2 else h_hi
                for s in range(HT):
                    last = pe.matmul(out_ap, w[:, p, s, :], v[:, sig, s:s + HALF],
                                     start=which == 0 and s == 0, stop=which == 2 and s == HT - 1)
                return last

            def dist(b, t):
                pe.matmul(bank_a[t % 2][:], da[:, t * 128:(t + 1) * 128], db[:], start=True, stop=True
                          ).then_inc(S["dist_mm"], 1)

            def gate(out_ap, g, src, v_hi, v_lo, start, stop):
                return passes(out_ap, gru_hi[:, 3 * src + g, :], gru_lo[:, 3 * src + g, :], v_hi, v_lo, start, stop)

            def step(b, par, first=False, last=False):
                n, t = b + 1, b - 1
                xh, xl = x1t_hi[par], x1t_lo[par]
                pe.wait_ge(S["x1t_out"], at(b, 2, 2))
                pe.wait_ge(S["x1t_lo_done"], b + 1)
                passes(bank_x[:], small_hi[:, 0, :], small_lo[:, 0, :], xh[:], xl[:]).then_inc(S["conv1_done"], 1)
                if not first:
                    pe.wait_ge(S["nm_lo_done"], b)
                passes(bank_y[:], small_hi[:, 1, :], small_lo[:, 1, :], xh[:], xl[:]).then_inc(S["se_done"], 1)
                if not first:
                    pe.wait_ge(S["ghn_done"], b)
                gate(bank_v[:], 2, 0, xh[:], xl[:], True, True).then_inc(S["ghn_mm"], 1)
                if not first:
                    pe.wait_ge(S["msgv_done"], b)
                for k in range(T):
                    tile = slice(k * 128, (k + 1) * 128)
                    ins = passes(bank_w[:, tile], xh[:, tile], xl[:, tile], small_hi[:, 2, :], small_lo[:, 2, :])
                ins.then_inc(S["msg_mm"], 1)
                pe.wait_ge(S["hhi_done"], b + 1)
                conv_part(b, 1, 0)
                conv_part(b, 1, 1)
                pe.wait_ge(S["hlo_done"], b + 1)
                conv_part(b, 1, 2)
                conv_part(b, 2, 0)
                pe.wait_ge(S["dadb_done"], b + 1)
                if not first:
                    pe.wait_ge(S["tr_done"], b)
                dist(b, 0)
                if not first:
                    pe.wait_ge(S["tz_done"], b)
                dist(b, 1)
                pe.wait_ge(S["q_done"], b + 1)
                if not last:
                    front_support(n)
                for k in (2, 3):
                    pe.wait_ge(S["exp_done"], at(b, T, k - 1))
                    dist(b, k)
                conv_part(b, 2, 1)
                if not last:
                    pe.wait_ge(S["h_done"], b + 1)
                    front_rows(n)
                conv_part(b, 2, 2)
                if not first:
                    pe.wait_ge(S["npre_done"], b)
                pe.wait_ge(S["slo_done"], b + 1)
                conv_part(b, 0, 0)
                conv_part(b, 0, 1)
                conv_part(b, 0, 2).then_inc(S["conv2_done"], 1)
                if not first:
                    pe.wait_ge(S["msgv_done"], b + 1)
                    tail_rows(t)
                pe.wait_ge(S["msglo_done"], b + 1)
                for k in range(T):
                    pe.wait_ge(S["amlo_done"], at(b, T, k + 1))
                    ins = passes(bank_y[:], msg_hi[:, k, :], msg_lo[:, k, :], am_hi[:, k, :], am_lo[:, k, :],
                                 start=k == 0, stop=k == T - 1)
                ins.then_inc(S["nmp_mm"], 1)
                pe.wait_ge(S["exp_done"], at(b, T, 4))
                gate(bank_a[0][:], 0, 0, xh[:], xl[:], True, False)
                gate(bank_a[1][:], 1, 0, xh[:], xl[:], True, False)
                pe.wait_ge(S["cv_done"], b + 1)
                pe.wait_ge(S["xc_lo_done"], b + 1)
                gate(bank_a[0][:], 0, 1, xc_hi[:], xc_lo[:], False, False)
                if not last:
                    front_x1t(n, 1 - par)
                gate(bank_a[1][:], 1, 1, xc_hi[:], xc_lo[:], False, False)
                gate(bank_p[:], 2, 1, xc_hi[:], xc_lo[:], True, False)
                pe.wait_ge(S["nm_lo_done"], b + 1)
                gate(bank_a[0][:], 0, 2, nm_hi[:], nm_lo[:], False, True).then_inc(S["r_mm"], 1)
                gate(bank_p[:], 2, 2, nm_hi[:], nm_lo[:], False, True).then_inc(S["n_mm"], 1)
                gate(bank_a[1][:], 1, 2, nm_hi[:], nm_lo[:], False, True).then_inc(S["z_mm"], 1)

            pe.wait_ge(S["prep_vec"], 64)
            front_support(0)
            front_rows(0)
            front_x1t(0, 0)
            pe.wait_ge(S["wsplit_lo"], 3)
            pe.wait_ge(S["pad_done"], 3)
            step(0, 0, first=True)
            with pe.Fori(1, B - 1, 2) as b:
                step(b, 1)
                step(b + 1, 0)
            step(B - 1, 1, last=True)
            tail_rows(B - 1)


def kernel(**inputs):
    import numpy as _np
    import concourse.bacc as _bacc
    from concourse import mybir as _mybir
    from concourse.bass_utils import run_bass_kernel_spmd as _run

    g = {k.removeprefix("L1_gnn_"): _np.asarray(v) for k, v in inputs.items()}
    se = _np.zeros((D, 128), _np.float32)
    b_se = _np.zeros(128, _np.float32)
    for group in range(4):
        for kind in range(3):
            at = 32 * group + SE * kind
            se[:, at:at + SE] = g["w_se"].T
            b_se[at:at + SE] = g["b_se"]
    gates = [g["w_hh"].T, g["w_ih"].T[0:D], g["w_ih"].T[D:2 * D]]
    arrays = {
        "x": g["x"],
        "adj_t": g["adj"].transpose(0, 2, 1),
        "w_conv2": g["conv2_w"].transpose(1, 2, 0),
        "w_gru": _np.stack([w[:, D * k:D * (k + 1)] for w in gates for k in range(3)], axis=1),
        "w_small": _np.stack([g["conv1_w"][:, :, 0].T, se, g["w_msg"].T], axis=1),
        "vectors": _np.stack([g["bn1_g"], g["bn1_b"], g["bn1_m"], g["bn1_v"], g["bn2_g"], g["bn2_b"], g["bn2_m"],
                              g["bn2_v"], *g["b_ih"].reshape(3, D), *g["b_hh"].reshape(3, D), b_se], axis=1),
        "b_msg": g["b_msg"],
        "rows_const": distance_rows(),
        "ident_in": _np.eye(128, dtype=_np.float32),
    }
    arrays = {k: _np.ascontiguousarray(v) for k, v in arrays.items()}
    nc = _bacc.Bacc("TRN2", target_bir_lowering=False, num_devices=1)
    args = [nc.dram_tensor(f"in_{k}", a.shape, _mybir.dt.from_np(a.dtype), kind="ExternalInput").ap()
            for k, a in arrays.items()]
    args.append(nc.dram_tensor("out_0", (B, N, D), _mybir.dt.float32, kind="ExternalOutput").ap())
    build(nc, *args)
    r = _run(nc, [{f"in_{k}": a for k, a in arrays.items()}], core_ids=[0])
    return r.results[0]["out_0"]
```

```python
from contextlib import ExitStack

import numpy as np

import concourse.bass as bass
from concourse import mybir

F32 = mybir.dt.float32
F32R = mybir.dt.float32r
ALU = mybir.AluOpType
ACT = mybir.ActivationFunctionType
AX = mybir.AxisListType

B, N, D = 16, 512, 128
T = N // 128
SE = 3
TAPS = 17
PAD = TAPS // 2
HT = (TAPS + 1) // 2
HALF = N // 2
HW = HALF + PAD
EPS = 1e-5
MIN_NORM = 1e-15
MAX_NORM = 1.0 - 0.004
ARTANH_MAX = float(np.float32(1 - 1e-07))
SERIES_BELOW = 0.25
SERIES = [1.0 / (2 * k + 1) for k in range(8)]

(V_G1, V_B1, V_M1, V_V1, V_G2, V_B2, V_M2, V_V2, V_IR, V_IZ, V_IN, V_HR, V_HZ, V_HN, V_SE) = range(15)
N_VEC = 15
(C_MU, C_NU, C_AA, C_BA, C_CA, C_AB, C_BB, C_CB) = range(8)
(W_SC1, W_BI1, W_SC2, W_BI2, W_HR, W_HZ, W_N, W_HHN, W_NU, W_T1, W_T2, W_T3, W_T4) = range(13)


def distance_rows():
    c = np.zeros((128, 8), np.float32)
    for p in range(128):
        group, row = p // 32, p % 32
        kind = row // SE if row < 3 * SE else 3
        low_a, low_b = group >= 2, group % 2 == 1
        c[p, C_MU] = kind in (1, 2)
        c[p, C_NU] = kind not in (1, 2)
        c[p, C_AA] = kind != 1
        c[p, C_BA] = -0.25 if kind == 1 else 0.0
        c[p, C_CA] = -1.0 if low_a and kind != 1 else 0.0
        c[p, C_AB] = kind != 2
        c[p, C_BB] = -0.25 if kind == 2 else 0.0
        c[p, C_CB] = -1.0 if low_b and kind != 2 else 0.0
    return c


def build(nc, x, adj_t, w_conv2, w_gru, w_small, vectors, b_msg, rows_const, ident_in, out):
    with ExitStack() as ctx:
        def sem(name):
            return ctx.enter_context(nc.semaphore(name))

        def sb(name, shape, dt=F32, where=ctx):
            return where.enter_context(nc.sbuf_tensor(name, shape, dt))

        def psum(name):
            return ctx.enter_context(nc.psum_tensor(name, [128, 512], F32))

        bank_a = [psum("bank_a0"), psum("bank_a1")]
        bank_c = psum("bank_c")
        bank_p = psum("bank_p")
        bank_x = psum("bank_x")
        bank_y = psum("bank_y")
        bank_w = psum("bank_w")
        bank_v = psum("bank_v")

        adj_sb = [sb(f"adj_sb{i}", [128, T, N]) for i in range(2)]
        adj_hi = sb("adj_hi", [128, T, N], F32R)
        adj_lo = sb("adj_lo", [128, T, N], F32R)
        conv_hi = sb("conv_hi", [128, 3, HT, 128], F32R)
        conv_lo = sb("conv_lo", [128, 3, HT, 128], F32R)
        gru_hi = sb("gru_hi", [128, 9, 128], F32R)
        gru_lo = sb("gru_lo", [128, 9, 128], F32R)
        small_hi = sb("small_hi", [128, 3, 128], F32R)
        small_lo = sb("small_lo", [128, 3, 128], F32R)
        ident = sb("ident", [128, 128])
        vec = sb("vec", [128, N_VEC])
        rows = sb("rows", [128, 8])
        der = sb("der", [128, 13])
        bmsg = sb("bmsg", [128, T, 128])
        neg_half_pow = sb("neg_half_pow", [128, T])
        art = sb("art", [128, (B + 1) * T])
        x_rows = [sb(f"x_rows{i}", [128, T, 128]) for i in range(2)]
        xt = sb("xt", [128, T, 128])
        xt_hi = sb("xt_hi", [128, T, 128], F32R)
        xt_lo = sb("xt_lo", [128, T, 128], F32R)
        supp = sb("supp", [128, N])
        supp_sq = sb("supp_sq", [128, T, 128])
        ss = sb("ss", [128, T])
        norm0 = sb("norm0", [128, T])
        norm = sb("norm", [128, T])
        rnorm = sb("rnorm", [128, T])
        th = sb("th", [128, T])
        fac = sb("fac", [128, T])
        y1 = sb("y1", [128, T, 128])
        st1 = sb("st1", [128, T, 6])
        mv1 = sb("mv1", [128, 3, T])
        ve1 = sb("ve1", [128, T])
        rstd1 = sb("rstd1", [128, T])
        x1_rows = [sb(f"x1_rows{i}", [128, T, 128]) for i in range(2)]
        x1t = [sb(f"x1t{i}", [128, N]) for i in range(2)]
        x1t_hi = [sb(f"x1t_hi{i}", [128, N], F32R) for i in range(2)]
        x1t_lo = [sb(f"x1t_lo{i}", [128, N], F32R) for i in range(2)]
        h = sb("h", [128, 3, HW])
        h_hi = sb("h_hi", [128, 3, HW], F32R)
        h_lo = sb("h_lo", [128, 3, HW], F32R)
        x1_bias = sb("x1_bias", [128, N])

        sm = [sb(f"sm{i}", [128, B * T]) for i in range(8)]
        pow_half = sb("pow_half", [128, B * T])
        nbias2 = sb("nbias2", [128, T])
        prep = ExitStack()
        EARLY = 2
        CHUNKS = [(2, 6), (6, 11), (11, B)]
        x_all = [sb(f"x_all{c}", [128, (b1 - b0) * T, 128], where=prep) for c, (b0, b1) in enumerate(CHUNKS)]
        x_sq = [sb(f"x_sq{i}", [128, T, 128], where=prep) for i in range(EARLY)]
        w2_st = sb("w2_st", [128, TAPS, 128], where=prep)
        filt = sb("filt", [128, 2, HT, 128], where=prep)
        gru_st = sb("gru_st", [128, 9, 128], where=prep)
        small_st = sb("small_st", [128, 3, 128], where=prep)
        prep.close()

        e = sb("e", [128, T, N])
        am_hi = sb("am_hi", [128, T, N], F32R)
        am_lo = sb("am_lo", [128, T, N], F32R)
        msg = sb("msg", [128, T, 128])
        msg_hi = sb("msg_hi", [128, T, 128], F32R)
        msg_lo = sb("msg_lo", [128, T, 128], F32R)
        s_mix = sb("s_mix", [128, N])
        q = sb("q", [128, N])
        q_hi = sb("q_hi", [128, N], F32R)
        ta = sb("ta", [128, N])
        tb = sb("tb", [128, N])
        da = sb("da", [128, N], F32R)
        db = sb("db", [128, N], F32R)
        cz = sb("cz", [128, N])
        cv = sb("cv", [128, N])
        xc_hi = sb("xc_hi", [128, N], F32R)
        xc_lo = sb("xc_lo", [128, N], F32R)
        nm_hi = sb("nm_hi", [128, N], F32R)
        nm_lo = sb("nm_lo", [128, N], F32R)
        tr = sb("tr", [128, N])
        tz = sb("tz", [128, N])
        ghn = sb("ghn", [128, N])
        un = sb("un", [128, N])
        nn = sb("nn", [128, N])
        xd = sb("xd", [128, N])
        o = sb("o", [128, N])
        y2 = sb("y2", [128, T, 128])
        st2 = sb("st2", [128, T, 6])
        mv2 = sb("mv2", [128, 3, T])
        ve2 = sb("ve2", [128, T])
        rstd2 = sb("rstd2", [128, T])
        y_out = [sb(f"y_out{i}", [128, T, 128]) for i in range(2)]

        names = """prep_x0 prep_x1 prep_x2 prep_rows prep_ident prep_bmsg prep_w2 prep_gru prep_small prep_vec adj_in0 adj_in1
            x_in0 x_in1 stored0 stored1
            sq_early sq_done ssum_early ssum_done ss_ready small_step root_done ln_done ln_ready art_done pool_const pad_done
            vec_step vec_eps vec_pow vec_done filt_done filt_split conv_hi_done gru_hi_done small_lo_done conv_lo_done gru_lo_done
            xt_done xt_hi_done xt_lo_done adj_hi_done adj_lo_done pow_ns pow_v1 pow_v2 xd_done
            conv1_done se_done msg_mm ghn_mm conv_p1 conv2_done dist_mm supp_mm srow_mm out_mm nmp_mm
            r_mm z_mm n_mm x1t_mm
            tr_done tz_done h_done smix_done small_hi_done nn_done msg_hi_done ghn_done tatb_done exp_done
            supp_out ss_done th_done xc_hi_done nm_hi_done x1t_out
            un_done npre_done hhi_done hlo_done hsum_done shi_done slo_done q_done qhi_done da_done dadb_done
            msgv_done msglo_done gate_done o_done am_done amhi_done amlo_done norm_done rnorm_done fac_done
            y1_done st1_done mv1_done ve1_done x1_done cz_done cv_done xc_lo_done
            y2_done st2_done mv2_done ve2_done nb2_done out_done nm_lo_done x1t_lo_done""".split()
        S = {n: sem(n) for n in names}

        def at(b, per, k):
            return b * per + k

        xr_dram = x.rearrange("b (t p) d -> b p t d", p=128)
        adj_dram = adj_t.rearrange("b (t p) i -> b p t i", p=128)
        out_dram = out.rearrange("b (t p) d -> b p t d", p=128)

        def row_of(dram, b):
            return dram[b] if isinstance(b, int) else dram[bass.ds(b, 1)].rearrange("a p t d -> (a p) t d")

        def cast_r(ap):
            return ap

        block = ctx.enter_context(nc.Block())

        @block.sync
        def _(sp):
            def load_x(b, par):
                sp.dma_start(x_rows[par][:], row_of(xr_dram, b)).then_inc(S[f"x_in{par}"], 16)

            def load_adj(b, par):
                sp.dma_start(adj_sb[par][:], row_of(adj_dram, b)).then_inc(S[f"adj_in{par}"], 16)

            def load(n, par):
                sp.wait_ge(S["y1_done"], at(n - 2, T, T))
                load_x(n, par)
                sp.wait_ge(S["am_done"], at(n - 2, T, T))
                sp.wait_ge(S["adj_lo_done"], at(n - 2, T, T))
                load_adj(n, par)

            def store(b, par):
                sp.wait_ge(S["out_done"], at(b, T, T))
                sp.dma_start(row_of(out_dram, b), y_out[par][:]).then_inc(S[f"stored{par}"], 16)

            sp.dma_start(vec[:], vectors).then_inc(S["prep_vec"], 16)
            sp.dma_start(rows[:], rows_const).then_inc(S["prep_rows"], 16)
            load_x(0, 0)
            load_x(1, 1)
            load_adj(0, 0)
            sp.dma_start(small_st[:], w_small).then_inc(S["prep_small"], 16)
            sp.dma_start(w2_st[:], w_conv2).then_inc(S["prep_w2"], 16)
            sp.dma_start(ident[:], ident_in).then_inc(S["prep_ident"], 16)
            sp.dma_start(gru_st[:], w_gru).then_inc(S["prep_gru"], 16)
            sp.dma_start(bmsg[:], b_msg.rearrange("(a c d) -> a c d", a=1, c=1).to_broadcast([128, T, 128])
                         ).then_inc(S["prep_bmsg"], 16)
            for c, (b0, b1) in enumerate(CHUNKS):
                sp.dma_start(x_all[c][:], x[b0:b1].rearrange("b (t p) d -> p (b t) d", p=128)
                             ).then_inc(S[f"prep_x{c}"], 16)
            load_adj(1, 1)
            load(2, 0)
            with sp.Fori(3, B - 1, 2) as n:
                load(n, 1)
                store(n - 3, 0)
                load(n + 1, 0)
                store(n - 2, 1)
            load(B - 1, 1)
            for b in range(B - 4, B):
                store(b, b % 2)
            for par in range(2):
                sp.wait_ge(S[f"stored{par}"], 16 * (B // 2))

        @block.gpsimd
        def _(pool):
            pool.memset(pow_half[:], 0.5).then_inc(S["pool_const"], 1)
            pool.memset(neg_half_pow[:], -0.5).then_inc(S["pool_const"], 1)
            pool.wait_ge(S["pool_const"], 2)
            pool.wait_ge(S["vec_eps"], 2)
            pool.tensor_tensor(der[:, W_T3:W_T3 + 2], der[:, W_T1:W_T1 + 2], neg_half_pow[:, 0:2], ALU.pow
                               ).then_inc(S["vec_pow"], 1)

            def roots(part, b0, b1):
                pool.wait_ge(S["ss_ready"], part)
                c = slice(b0 * T, b1 * T)
                pool.tensor_tensor(sm[1][:, c], sm[0][:, c], pow_half[:, c], ALU.pow).then_inc(S["root_done"], 1)

            def xt_split(n, par, turn):
                pool.wait_ge(S[f"x_in{par}"], turn)
                if isinstance(n, int):
                    pool.wait_ge(S["art_done"], 1 if n < EARLY else 2)
                if not (isinstance(n, int) and n == 0):
                    pool.wait_ge(S["supp_mm"], n)
                a = art[:, n * T:(n + 1) * T] if isinstance(n, int) else art[:, bass.ds(n * T, T)]
                a_all = a.unsqueeze(2).to_broadcast([128, T, 128])
                pool.tensor_tensor(xt[:], x_rows[par][:], a_all, ALU.mult).then_inc(S["xt_done"], 1)
                pool.tensor_tensor(xt_hi[:], x_rows[par][:], a_all, ALU.mult).then_inc(S["xt_hi_done"], 1)
                pool.wait_ge(S["xt_done"], n + 1)
                pool.wait_ge(S["xt_hi_done"], n + 1)
                pool.tensor_tensor(xt_lo[:], xt[:], xt_hi[:].bitcast(F32), ALU.subtract).then_inc(S["xt_lo_done"], 1)

            def adj_low(n, par):
                for t in range(T):
                    pool.wait_ge(S["adj_hi_done"], at(n, T, t + 1))
                    pool.tensor_tensor(adj_lo[:, t, :], adj_sb[par][:, t, :], adj_hi[:, t, :].bitcast(F32),
                                       ALU.subtract).then_inc(S["adj_lo_done"], 1)

            def front_pows(n):
                pool.wait_ge(S["ss_done"], at(n, T, T))
                pool.tensor_tensor(norm0[:], ss[:], pow_half[:, 0:T], ALU.pow).then_inc(S["pow_ns"], 1)
                pool.wait_ge(S["ve1_done"], n + 1)
                pool.tensor_tensor(rstd1[:], ve1[:], neg_half_pow[:], ALU.pow).then_inc(S["pow_v1"], 1)

            def tail_xd(t, par):
                pool.wait_ge(S["nn_done"], t + 1)
                pool.tensor_tensor(xd[:], x1t[par][:], nn[:], ALU.subtract).then_inc(S["xd_done"], 1)

            def tail_pow(t):
                pool.wait_ge(S["ve2_done"], t + 1)
                pool.tensor_tensor(rstd2[:], ve2[:], neg_half_pow[:], ALU.pow).then_inc(S["pow_v2"], 1)

            def step(b, par, first=False, front=True, ahead=None):
                n, t = b + 1, b - 1
                if not first:
                    tail_xd(t, 1 - par)
                if front:
                    front_pows(n)
                if ahead is not None:
                    xt_split(b + 2, par, ahead)
                if not first:
                    tail_pow(t)
                if ahead is not None:
                    adj_low(b + 2, par)

            roots(1, 0, EARLY)
            adj_low(0, 0)
            xt_split(0, 0, 16)
            front_pows(0)
            xt_split(1, 1, 16)
            adj_low(1, 1)
            roots(2, EARLY, B)
            step(0, 0, first=True, ahead=32)
            with pool.Fori(1, B - 3, 2) as b:
                step(b, 1, ahead=8 * b + 24)
                step(b + 1, 0, ahead=8 * b + 40)
            step(B - 3, 1, ahead=16 * (B // 2))
            step(B - 2, 0)
            step(B - 1, 1, front=False)
            tail_xd(B - 1, 1)
            tail_pow(B - 1)

        @block.scalar
        def _(act):
            act.wait_ge(S["x_in0"], 16)
            act.activation(x_sq[0][:], x_rows[0][:], ACT.Square).then_inc(S["sq_early"], 1)
            act.wait_ge(S["x_in1"], 16)
            act.activation(x_sq[1][:], x_rows[1][:], ACT.Square).then_inc(S["sq_early"], 1)

            def logs(part, b0, b1):
                act.wait_ge(S["ln_ready"], part)
                c = slice(b0 * T, b1 * T)
                act.activation(sm[5][:, c], sm[4][:, c], ACT.Ln).then_inc(S["ln_done"], 1)

            def adj_high(n, par, turn):
                act.wait_ge(S[f"adj_in{par}"], turn)
                if not (isinstance(n, int) and n == 0):
                    act.wait_ge(S["supp_mm"], n)
                for t in range(T):
                    act.activation(adj_hi[:, t, :], adj_sb[par][:, t, :], ACT.Copy).then_inc(S["adj_hi_done"], 1)

            def front_support(n):
                act.wait_ge(S["supp_mm"], n + 1)
                act.activation(supp[:], bank_p[:], ACT.Copy).then_inc(S["supp_out"], 1)

            def front_squares(n):
                act.wait_ge(S["srow_mm"], n + 1)
                for t in range(T):
                    act.activation(supp_sq[:, t, :], bank_x[:, t * 128:(t + 1) * 128], ACT.Square,
                                   accum_out=ss[:, t:t + 1]).then_inc(S["ss_done"], 1)

            def front_tanh(n):
                act.wait_ge(S["norm_done"], n + 1)
                act.activation(th[:], norm[:], ACT.Tanh).then_inc(S["th_done"], 1)

            def front_x1t(n, par):
                act.wait_ge(S["x1t_mm"], n + 1)
                act.activation(x1t_hi[par][:], bank_x[:], ACT.Copy)
                act.activation(x1t[par][:], bank_x[:], ACT.Copy).then_inc(S["x1t_out"], 1)
                act.activation(x1_bias[:], bank_x[:], ACT.Identity, bias=der[:, W_BI2:W_BI2 + 1]
                               ).then_inc(S["x1t_out"], 1)

            def tail_rz(t):
                act.wait_ge(S["r_mm"], t + 1)
                act.activation(tr[:], bank_a[0][:], ACT.Tanh, bias=der[:, W_HR:W_HR + 1], scale=0.5
                               ).then_inc(S["tr_done"], 1)
                act.wait_ge(S["z_mm"], t + 1)
                act.activation(tz[:], bank_a[1][:], ACT.Tanh, bias=der[:, W_HZ:W_HZ + 1], scale=0.5
                               ).then_inc(S["tz_done"], 1)

            def tail_n(t):
                act.wait_ge(S["npre_done"], t + 1)
                act.activation(nn[:], un[:], ACT.Tanh, bias=vec[:, V_IN:V_IN + 1]).then_inc(S["nn_done"], 1)

            def main_h(b):
                act.wait_ge(S["conv1_done"], b + 1)
                act.activation(h[:, 0:2, PAD // 2:PAD // 2 + HALF], bank_x[:].rearrange("p (m g) -> p g m", g=2),
                               ACT.Relu, bias=der[:, W_BI1:W_BI1 + 1], scale=der[:, W_SC1:W_SC1 + 1]
                               ).then_inc(S["h_done"], 1)

            def main_mix(b):
                act.wait_ge(S["se_done"], b + 1)
                act.activation(s_mix[:], bank_y[:], ACT.Identity, bias=der[:, W_NU:W_NU + 1],
                               scale=rows[:, C_MU:C_MU + 1]).then_inc(S["smix_done"], 1)

            def main_ghn(b):
                act.wait_ge(S["ghn_mm"], b + 1)
                act.activation(ghn[:], bank_v[:], ACT.Identity, bias=der[:, W_HHN:W_HHN + 1], scale=0.5
                               ).then_inc(S["ghn_done"], 1)

            def main_msg(b):
                act.wait_ge(S["msgv_done"], b + 1)
                act.activation(msg_hi[:], msg[:], ACT.Relu).then_inc(S["msg_hi_done"], 1)

            def main_tab(b):
                act.wait_ge(S["q_done"], b + 1)
                act.activation(ta[:], q[:], ACT.Identity, bias=rows[:, C_BA:C_BA + 1], scale=rows[:, C_AA:C_AA + 1]
                               ).then_inc(S["tatb_done"], 1)
                act.activation(tb[:], q[:], ACT.Identity, bias=rows[:, C_BB:C_BB + 1], scale=rows[:, C_AB:C_AB + 1]
                               ).then_inc(S["tatb_done"], 1)

            def main_exp(b, t):
                act.wait_ge(S["dist_mm"], at(b, T, t + 1))
                act.activation(e[:, t, :], bank_a[t % 2][:], ACT.Exp, scale=2.0).then_inc(S["exp_done"], 1)

            def main_amhi(b, t):
                act.wait_ge(S["am_done"], at(b, T, t + 1))
                act.activation(am_hi[:, t, :], e[:, t, :], ACT.Copy).then_inc(S["amhi_done"], 1)

            def main_conv_hi(b):
                act.wait_ge(S["cv_done"], b + 1)
                act.activation(xc_hi[:], cv[:], ACT.Relu).then_inc(S["xc_hi_done"], 1)

            def main_nm_hi(b):
                act.wait_ge(S["nmp_mm"], b + 1)
                act.activation(nm_hi[:], bank_y[:], ACT.Copy).then_inc(S["nm_hi_done"], 1)

            def tail_out(t, par, stored):
                act.wait_ge(S["nb2_done"], t + 1)
                if stored is not None:
                    act.wait_ge(S[f"stored{par}"], stored)
                for k in range(T):
                    act.activation(y_out[par][:, k, :], y2[:, k, :], ACT.Identity, bias=nbias2[:, k:k + 1],
                                   scale=rstd2[:, k:k + 1]).then_inc(S["out_done"], 1)

            def step(b, par, first=False, front=True, ahead=None, stored=None):
                n, t = b + 1, b - 1
                if not first:
                    tail_rz(t)
                main_h(b)
                main_mix(b)
                if not first:
                    tail_n(t)
                main_tab(b)
                main_msg(b)
                main_ghn(b)
                if front:
                    front_support(n)
                main_exp(b, 0)
                main_exp(b, 1)
                if front:
                    front_squares(n)
                main_amhi(b, 0)
                main_amhi(b, 1)
                main_exp(b, 2)
                main_exp(b, 3)
                if front:
                    front_tanh(n)
                main_amhi(b, 2)
                main_amhi(b, 3)
                if first:
                    logs(2, EARLY, B)
                main_conv_hi(b)
                main_nm_hi(b)
                if front:
                    front_x1t(n, 1 - par)
                if ahead is not None:
                    adj_high(b + 2, par, ahead)
                if not first:
                    tail_out(t, 1 - par, stored)

            logs(1, 0, EARLY)
            adj_high(0, 0, 16)
            act.wait_ge(S["prep_small"], 16)
            act.activation(small_hi[:], small_st[:], ACT.Copy).then_inc(S["small_hi_done"], 1)
            act.wait_ge(S["filt_split"], 1)
            act.activation(conv_hi[:, 1:3, :, :], filt[:], ACT.Copy).then_inc(S["conv_hi_done"], 1)
            act.activation(conv_hi[:, 0, :, :], w2_st[:, 0:TAPS:2, :], ACT.Copy).then_inc(S["conv_hi_done"], 1)
            act.wait_ge(S["prep_gru"], 16)
            act.activation(gru_hi[:], gru_st[:], ACT.Copy).then_inc(S["gru_hi_done"], 1)
            for c in range(len(CHUNKS)):
                act.wait_ge(S[f"prep_x{c}"], 16)
                act.activation(x_all[c][:], x_all[c][:], ACT.Square).then_inc(S["sq_done"], 1)
                if c == 0:
                    front_support(0)
                    front_squares(0)
                    front_tanh(0)
            act.wait_ge(S["vec_done"], 1)
            front_x1t(0, 0)
            adj_high(1, 1, 16)
            step(0, 0, first=True, ahead=32)
            step(1, 1, ahead=32)
            step(2, 0, ahead=48)
            with act.Fori(3, B - 3, 2) as b:
                step(b, 1, ahead=8 * b + 24, stored=8 * b - 8)
                step(b + 1, 0, ahead=8 * b + 40, stored=8 * b - 8)
            step(B - 3, 1, ahead=16 * (B // 2), stored=8 * (B - 3) - 8)
            step(B - 2, 0, stored=8 * (B - 3) - 8)
            step(B - 1, 1, front=False, stored=8 * (B - 1) - 8)
            tail_rz(B - 1)
            tail_n(B - 1)
            tail_out(B - 1, 1, 8 * (B - 1) - 8)

        @block.vector
        def _(dve):
            steps = [0]

            def small(ins):
                steps[0] += 1
                ins.then_inc(S["small_step"], 1)
                dve.wait_ge(S["small_step"], steps[0])

            for buf in (h, h_hi, h_lo):
                v = buf[:] if buf is h else buf[:].bitcast(F32)
                dve.memset(v[:, :, 0:PAD // 2], 0.0)
                dve.memset(v[:, :, PAD // 2 + HALF:HW], 0.0).then_inc(S["pad_done"], 1)

            dve.wait_ge(S["prep_vec"], 16)
            dve.wait_ge(S["prep_rows"], 16)
            dve.tensor_scalar(der[:, W_T1:W_T1 + 1], vec[:, V_V1:V_V1 + 1], EPS, None, ALU.add).then_inc(S["vec_eps"], 1)
            dve.tensor_scalar(der[:, W_T2:W_T2 + 1], vec[:, V_V2:V_V2 + 1], EPS, None, ALU.add).then_inc(S["vec_eps"], 1)

            def roots_in(part, b0, b1):
                c = slice(b0 * T, b1 * T)
                dve.tensor_scalar(sm[0][:, c], sm[0][:, c], MIN_NORM * MIN_NORM, None, ALU.max
                                  ).then_inc(S["ss_ready"], 1)

            def log_in(part, b0, b1):
                c = slice(b0 * T, b1 * T)
                dve.wait_ge(S["root_done"], part)
                small(dve.tensor_scalar(sm[2][:, c], sm[1][:, c], MIN_NORM, None, ALU.max))
                small(dve.tensor_scalar(sm[3][:, c], sm[2][:, c], ARTANH_MAX, None, ALU.min))
                small(dve.tensor_scalar(sm[6][:, c], sm[3][:, c], -1.0, 1.0, ALU.mult, ALU.add))
                small(dve.reciprocal(sm[6][:, c], sm[6][:, c]))
                dve.tensor_scalar(sm[7][:, c], sm[3][:, c], SERIES_BELOW, None, ALU.is_lt)
                dve.scalar_tensor_tensor(sm[4][:, c], sm[3][:, c], 1.0, sm[6][:, c], ALU.add, ALU.mult
                                         ).then_inc(S["ln_ready"], 1)
                dve.wait_ge(S["ln_ready"], part)
                small(dve.tensor_tensor(sm[3][:, c], sm[3][:, c], sm[3][:, c], ALU.mult))
                small(dve.tensor_scalar(sm[6][:, c], sm[3][:, c], SERIES[-1], None, ALU.mult))
                for k in SERIES[-2:0:-1]:
                    small(dve.scalar_tensor_tensor(sm[6][:, c], sm[6][:, c], k, sm[3][:, c], ALU.add, ALU.mult))
                small(dve.tensor_scalar(sm[6][:, c], sm[6][:, c], SERIES[0], None, ALU.add))
                small(dve.reciprocal(sm[2][:, c], sm[2][:, c]))

            def art_out(part, b0, b1):
                c = slice(b0 * T, b1 * T)
                dve.wait_ge(S["ln_done"], part)
                small(dve.scalar_tensor_tensor(sm[5][:, c], sm[5][:, c], 0.5, sm[2][:, c], ALU.mult, ALU.mult))
                small(dve.tensor_tensor(sm[6][:, c], sm[6][:, c], sm[5][:, c], ALU.subtract))
                small(dve.tensor_tensor(sm[6][:, c], sm[6][:, c], sm[7][:, c], ALU.mult))
                dve.tensor_tensor(art[:, c], sm[5][:, c], sm[6][:, c], ALU.add).then_inc(S["art_done"], 1)

            for i in range(EARLY):
                dve.wait_ge(S["sq_early"], i + 1)
                dve.tensor_reduce(sm[0][:, i * T:(i + 1) * T], x_sq[i][:], AX.X, ALU.add).then_inc(S["ssum_early"], 1)
            dve.wait_ge(S["ssum_early"], EARLY)
            roots_in(1, 0, EARLY)
            small(dve.tensor_tensor(der[:, W_HR:W_HR + 2], vec[:, V_IR:V_IR + 2], vec[:, V_HR:V_HR + 2], ALU.add))
            small(dve.tensor_scalar(der[:, W_HR:W_HR + 2], der[:, W_HR:W_HR + 2], 0.5, None, ALU.mult))
            small(dve.tensor_scalar(der[:, W_HHN:W_HHN + 1], vec[:, V_HN:V_HN + 1], 0.5, None, ALU.mult))
            small(dve.tensor_tensor(der[:, W_NU:W_NU + 1], vec[:, V_SE:V_SE + 1], rows[:, C_MU:C_MU + 1], ALU.mult))
            small(dve.tensor_tensor(der[:, W_NU:W_NU + 1], der[:, W_NU:W_NU + 1], rows[:, C_NU:C_NU + 1], ALU.add))
            log_in(1, 0, EARLY)
            art_out(1, 0, EARLY)
            dve.wait_ge(S["vec_pow"], 1)
            for k, (g, bb, m, sc, bi) in enumerate(((V_G1, V_B1, V_M1, W_SC1, W_BI1), (V_G2, V_B2, V_M2, W_SC2, W_BI2))):
                small(dve.tensor_tensor(der[:, sc:sc + 1], vec[:, g:g + 1], der[:, W_T3 + k:W_T3 + k + 1], ALU.mult))
                small(dve.tensor_tensor(der[:, bi:bi + 1], vec[:, m:m + 1], der[:, sc:sc + 1], ALU.mult))
                ins = dve.tensor_tensor(der[:, bi:bi + 1], vec[:, bb:bb + 1], der[:, bi:bi + 1], ALU.subtract)
            ins.then_inc(S["vec_done"], 1)
            dve.wait_ge(S["prep_w2"], 16)
            even = w2_st[:, 0:TAPS:2, :]
            odd = w2_st[:, 1:TAPS:2, :]
            dve.tensor_tensor(filt[:, 0, 0:HT - 1, :], odd, even[:, 0:HT - 1, :], ALU.subtract)
            dve.tensor_scalar(filt[:, 0, HT - 1, :], even[:, HT - 1, :], -1.0, None, ALU.mult)
            dve.tensor_tensor(filt[:, 1, 1:HT, :], odd, even[:, 1:HT, :], ALU.subtract)
            dve.tensor_scalar(filt[:, 1, 0, :], even[:, 0, :], -1.0, None, ALU.mult).then_inc(S["filt_split"], 1)
            dve.wait_ge(S["small_hi_done"], 1)
            dve.tensor_tensor(small_lo[:], small_st[:], small_hi[:].bitcast(F32), ALU.subtract).then_inc(S["small_lo_done"], 1)
            dve.wait_ge(S["conv_hi_done"], 1)
            dve.tensor_tensor(conv_lo[:, 1:3, :, :], filt[:], conv_hi[:, 1:3, :, :].bitcast(F32), ALU.subtract)
            dve.wait_ge(S["conv_hi_done"], 2)
            dve.tensor_tensor(conv_lo[:, 0, :, :], even, conv_hi[:, 0, :, :].bitcast(F32), ALU.subtract
                              ).then_inc(S["conv_lo_done"], 1)

            def front_factor(n):
                dve.wait_ge(S["pow_ns"], n + 1)
                dve.tensor_scalar(norm[:], norm0[:], MIN_NORM, None, ALU.max).then_inc(S["norm_done"], 1)
                dve.wait_ge(S["norm_done"], n + 1)
                dve.reciprocal(rnorm[:], norm[:]).then_inc(S["rnorm_done"], 1)
                dve.wait_ge(S["rnorm_done"], n + 1)
                dve.wait_ge(S["th_done"], n + 1)
                dve.scalar_tensor_tensor(fac[:], th[:], MAX_NORM, rnorm[:], ALU.min, ALU.mult).then_inc(S["fac_done"], 1)

            def front_y1(n, par):
                dve.wait_ge(S["fac_done"], n + 1)
                for t in range(T):
                    dve.scalar_tensor_tensor(y1[:, t, :], bank_x[:, t * 128:(t + 1) * 128], fac[:, t:t + 1],
                                             x_rows[par][:, t, :], ALU.mult, ALU.add).then_inc(S["y1_done"], 1)

            def stats(y, st, mv, ve, b, y_sem, y_per, st_sem, mv_sem, ve_sem):
                for t in range(T):
                    dve.wait_ge(S[y_sem], at(b, y_per, min(t + 1, y_per)))
                    dve.bn_stats(st[:, t, :], y[:, t, :]).then_inc(S[st_sem], 1)
                dve.wait_ge(S[st_sem], at(b, T, T))
                dve.tensor_tensor(mv[:, 0, :], st[:, :, 1], st[:, :, 4], ALU.add)
                dve.tensor_tensor(mv[:, 1, :], st[:, :, 1], st[:, :, 4], ALU.subtract)
                dve.tensor_tensor(mv[:, 2, :], st[:, :, 2], st[:, :, 5], ALU.add).then_inc(S[mv_sem], 1)
                dve.wait_ge(S[mv_sem], at(b, 2, 1))
                dve.tensor_scalar(mv[:, 0, :], mv[:, 0, :], 0.5, None, ALU.mult)
                dve.scalar_tensor_tensor(mv[:, 1, :], mv[:, 1, :], 0.25, mv[:, 1, :], ALU.mult, ALU.mult)
                dve.tensor_scalar(mv[:, 2, :], mv[:, 2, :], 1.0 / D, EPS, ALU.mult, ALU.add).then_inc(S[mv_sem], 1)
                dve.wait_ge(S[mv_sem], at(b, 2, 2))
                dve.tensor_tensor(ve[:], mv[:, 1, :], mv[:, 2, :], ALU.add).then_inc(S[ve_sem], 1)

            def front_x1(n, par):
                if not (isinstance(n, int) and n < 2):
                    dve.wait_ge(S["y2_done"], n - 1)
                dve.wait_ge(S["pow_v1"], n + 1)
                for t in range(T):
                    dve.tensor_scalar(x1_rows[par][:, t, :], y1[:, t, :], mv1[:, 0, t:t + 1], rstd1[:, t:t + 1],
                                      ALU.subtract, ALU.mult).then_inc(S["x1_done"], 1)

            def front_x1lo(n, par):
                dve.wait_ge(S["x1t_out"], at(n, 2, 1))
                dve.tensor_tensor(x1t_lo[par][:], x1t[par][:], x1t_hi[par][:].bitcast(F32), ALU.subtract
                                  ).then_inc(S["x1t_lo_done"], 1)

            def tail_un(t):
                dve.wait_ge(S["tr_done"], t + 1)
                dve.wait_ge(S["ghn_done"], t + 1)
                dve.scalar_tensor_tensor(un[:], tr[:], 1.0, ghn[:], ALU.add, ALU.mult).then_inc(S["un_done"], 1)
                dve.wait_ge(S["un_done"], t + 1)
                dve.wait_ge(S["n_mm"], t + 1)
                dve.tensor_tensor(un[:], bank_p[:], un[:], ALU.add).then_inc(S["npre_done"], 1)

            def tail_o(t):
                dve.wait_ge(S["xd_done"], t + 1)
                dve.wait_ge(S["tz_done"], t + 1)
                dve.scalar_tensor_tensor(xd[:], tz[:], 1.0, xd[:], ALU.add, ALU.mult).then_inc(S["gate_done"], 1)
                dve.wait_ge(S["gate_done"], t + 1)
                dve.scalar_tensor_tensor(o[:], xd[:], 0.5, nn[:], ALU.mult, ALU.add).then_inc(S["o_done"], 1)

            def tail_y2(t, par):
                dve.wait_ge(S["out_mm"], t + 1)
                dve.tensor_tensor(y2[:], bank_w[:].rearrange("p (t d) -> p t d", t=T), x1_rows[par][:], ALU.add
                                  ).then_inc(S["y2_done"], 1)

            def tail_stats(t):
                stats(y2, st2, mv2, ve2, t, "y2_done", 1, "st2_done", "mv2_done", "ve2_done")

            def tail_bias(t):
                dve.wait_ge(S["pow_v2"], t + 1)
                dve.scalar_tensor_tensor(nbias2[:], mv2[:, 0, :], -1.0, rstd2[:], ALU.mult, ALU.mult
                                         ).then_inc(S["nb2_done"], 1)

            def main_h(b):
                dve.wait_ge(S["h_done"], b + 1)
                dve.tensor_copy(h_hi[:, 0:2, :], h[:, 0:2, :]).then_inc(S["hhi_done"], 1)
                dve.wait_ge(S["hhi_done"], b + 1)
                dve.tensor_tensor(h_lo[:, 0:2, :], h[:, 0:2, :], h_hi[:, 0:2, :].bitcast(F32), ALU.subtract
                                  ).then_inc(S["hlo_done"], 1)
                dve.tensor_tensor(h[:, 2, :], h[:, 0, :], h[:, 1, :], ALU.add).then_inc(S["hsum_done"], 1)
                dve.wait_ge(S["hsum_done"], b + 1)
                dve.tensor_copy(h_hi[:, 2, :], h[:, 2, :]).then_inc(S["shi_done"], 1)
                dve.wait_ge(S["shi_done"], b + 1)
                dve.tensor_tensor(h_lo[:, 2, :], h[:, 2, :], h_hi[:, 2, :].bitcast(F32), ALU.subtract
                                  ).then_inc(S["slo_done"], 1)

            def main_q(b):
                dve.wait_ge(S["smix_done"], b + 1)
                dve.scalar_tensor_tensor(q[:], bank_y[:], vec[:, V_SE:V_SE + 1], s_mix[:], ALU.add, ALU.mult
                                         ).then_inc(S["q_done"], 1)
                dve.wait_ge(S["q_done"], b + 1)
                dve.tensor_copy(q_hi[:], q[:]).then_inc(S["qhi_done"], 1)

            def main_dab(b):
                dve.wait_ge(S["qhi_done"], b + 1)
                dve.wait_ge(S["tatb_done"], at(b, 2, 2))
                dve.scalar_tensor_tensor(da[:], q_hi[:].bitcast(F32), rows[:, C_CA:C_CA + 1], ta[:], ALU.mult, ALU.add
                                         ).then_inc(S["da_done"], 1)
                dve.scalar_tensor_tensor(db[:], q_hi[:].bitcast(F32), rows[:, C_CB:C_CB + 1], tb[:], ALU.mult, ALU.add
                                         ).then_inc(S["dadb_done"], 1)

            def main_msgv(b):
                if isinstance(b, int) and b == 0:
                    dve.wait_ge(S["prep_bmsg"], 16)
                dve.wait_ge(S["msg_mm"], b + 1)
                dve.tensor_tensor(msg[:], bank_w[:].rearrange("p (t d) -> p t d", t=T), bmsg[:], ALU.add
                                  ).then_inc(S["msgv_done"], 1)

            def main_msglo(b):
                dve.wait_ge(S["msg_hi_done"], b + 1)
                dve.scalar_tensor_tensor(msg_lo[:], msg[:], 0.0, msg_hi[:].bitcast(F32), ALU.max, ALU.subtract
                                         ).then_inc(S["msglo_done"], 1)

            def main_am(b, par, t):
                dve.wait_ge(S["exp_done"], at(b, T, t + 1))
                dve.tensor_tensor(e[:, t, :], e[:, t, :], adj_sb[par][:, t, :], ALU.mult).then_inc(S["am_done"], 1)

            def main_amlo(b, t):
                dve.wait_ge(S["amhi_done"], at(b, T, t + 1))
                dve.tensor_tensor(am_lo[:, t, :], e[:, t, :], am_hi[:, t, :].bitcast(F32), ALU.subtract
                                  ).then_inc(S["amlo_done"], 1)

            def main_conv(b):
                dve.wait_ge(S["conv2_done"], b + 1)
                dve.wait_ge(S["x1t_out"], at(b, 2, 2))
                xb = x1_bias[:].rearrange("p (m g) -> p g m", g=2)
                zv = cz[:].rearrange("p (g m) -> p g m", g=2)
                for g in range(2):
                    ins = dve.scalar_tensor_tensor(zv[:, g, :], bank_p[:, 0:HALF], der[:, W_SC2:W_SC2 + 1],
                                                   xb[:, g, :], ALU.mult, ALU.add)
                ins.then_inc(S["cz_done"], 1)
                dve.wait_ge(S["cz_done"], b + 1)
                dve.scalar_tensor_tensor(cv[:].rearrange("p (m g) -> p g m", g=2),
                                         bank_c[:].rearrange("p (g m) -> p g m", g=2), der[:, W_SC2:W_SC2 + 1],
                                         zv, ALU.mult, ALU.add).then_inc(S["cv_done"], 1)

            def main_conv_lo(b):
                dve.wait_ge(S["xc_hi_done"], b + 1)
                dve.scalar_tensor_tensor(xc_lo[:], cv[:], 0.0, xc_hi[:].bitcast(F32), ALU.max, ALU.subtract
                                         ).then_inc(S["xc_lo_done"], 1)

            def main_nm_lo(b):
                dve.wait_ge(S["nm_hi_done"], b + 1)
                dve.tensor_tensor(nm_lo[:], bank_y[:], nm_hi[:].bitcast(F32), ALU.subtract).then_inc(S["nm_lo_done"], 1)

            def step(b, par, first=False, front=True):
                n, t = b + 1, b - 1
                if not first:
                    tail_un(t)
                main_h(b)
                main_q(b)
                main_msgv(b)
                main_dab(b)
                if not first:
                    tail_o(t)
                main_msglo(b)
                main_am(b, par, 0)
                main_am(b, par, 1)
                main_amlo(b, 0)
                if front:
                    front_factor(n)
                    front_y1(n, 1 - par)
                    stats(y1, st1, mv1, ve1, n, "y1_done", T, "st1_done", "mv1_done", "ve1_done")
                main_am(b, par, 2)
                main_am(b, par, 3)
                if not first:
                    tail_y2(t, 1 - par)
                main_amlo(b, 1)
                main_amlo(b, 2)
                if front:
                    front_x1(n, 1 - par)
                main_amlo(b, 3)
                if first:
                    dve.wait_ge(S["ssum_done"], len(CHUNKS))
                    art_out(2, EARLY, B)
                main_conv(b)
                main_conv_lo(b)
                if not first:
                    tail_stats(t)
                main_nm_lo(b)
                if front:
                    front_x1lo(n, 1 - par)
                if not first:
                    tail_bias(t)

            for c, (b0, b1) in enumerate(CHUNKS):
                dve.wait_ge(S["sq_done"], c + 1)
                dve.tensor_reduce(sm[0][:, b0 * T:b1 * T], x_all[c][:], AX.X, ALU.add).then_inc(S["ssum_done"], 1)
                if c == 0:
                    front_factor(0)
                    front_y1(0, 0)
                    stats(y1, st1, mv1, ve1, 0, "y1_done", T, "st1_done", "mv1_done", "ve1_done")
                    front_x1(0, 0)
            dve.wait_ge(S["ssum_done"], len(CHUNKS))
            roots_in(2, EARLY, B)
            front_x1lo(0, 0)
            dve.wait_ge(S["gru_hi_done"], 1)
            dve.tensor_tensor(gru_lo[:], gru_st[:], gru_hi[:].bitcast(F32), ALU.subtract).then_inc(S["gru_lo_done"], 1)
            log_in(2, EARLY, B)
            step(0, 0, first=True)
            with dve.Fori(1, B - 1, 2) as b:
                step(b, 1)
                step(b + 1, 0)
            step(B - 1, 1, front=False)
            tail_un(B - 1)
            tail_o(B - 1)
            tail_y2(B - 1, 1)
            tail_stats(B - 1)
            tail_bias(B - 1)

        @block.tensor
        def _(pe):
            def passes(out_ap, w_hi, w_lo, v_hi, v_lo, start=True, stop=True):
                pe.matmul(out_ap, w_hi, v_hi, start=start, stop=False)
                pe.matmul(out_ap, w_lo, v_hi, start=False, stop=False)
                return pe.matmul(out_ap, w_hi, v_lo, start=False, stop=stop)

            def front_support(n):
                pe.wait_ge(S["xt_lo_done"], n + 1)
                for t in range(T):
                    pe.wait_ge(S["adj_lo_done"], at(n, T, t + 1))
                    last = passes(bank_p[:], xt_hi[:, t, :], xt_lo[:, t, :], adj_hi[:, t, :], adj_lo[:, t, :],
                                  start=t == 0, stop=t == T - 1)
                last.then_inc(S["supp_mm"], 1)

            def front_rows(n):
                pe.wait_ge(S["supp_out"], n + 1)
                for t in range(T):
                    last = pe.transpose(bank_x[:, t * 128:(t + 1) * 128], supp[:, t * 128:(t + 1) * 128], ident[:])
                last.then_inc(S["srow_mm"], 1)

            def front_x1t(n, par):
                for t in range(T):
                    pe.wait_ge(S["x1_done"], at(n, T, t + 1))
                    last = pe.transpose(bank_x[:, t * 128:(t + 1) * 128], x1_rows[par][:, t, :], ident[:])
                last.then_inc(S["x1t_mm"], 1)

            def tail_rows(t):
                pe.wait_ge(S["o_done"], t + 1)
                for k in range(T):
                    last = pe.transpose(bank_w[:, k * 128:(k + 1) * 128], o[:, k * 128:(k + 1) * 128], ident[:])
                last.then_inc(S["out_mm"], 1)

            def conv_part(b, p, which):
                out_ap = (bank_p[:, 0:HALF], bank_c[:, 0:HALF], bank_c[:, HALF:N])[p]
                sig = (2, 1, 0)[p]
                w = conv_lo if which == 1 else conv_hi
                v = h_lo if which == 2 else h_hi
                for s in range(HT):
                    last = pe.matmul(out_ap, w[:, p, s, :], v[:, sig, s:s + HALF],
                                     start=which == 0 and s == 0, stop=which == 2 and s == HT - 1)
                return last

            def dist(b, t):
                pe.matmul(bank_a[t % 2][:], da[:, t * 128:(t + 1) * 128], db[:], start=True, stop=True
                          ).then_inc(S["dist_mm"], 1)

            def gate(out_ap, g, src, v_hi, v_lo, start, stop):
                return passes(out_ap, gru_hi[:, 3 * src + g, :], gru_lo[:, 3 * src + g, :], v_hi, v_lo, start, stop)

            def step(b, par, first=False, front=True):
                n, t = b + 1, b - 1
                xh, xl = x1t_hi[par], x1t_lo[par]
                pe.wait_ge(S["x1t_out"], at(b, 2, 2))
                pe.wait_ge(S["x1t_lo_done"], b + 1)
                passes(bank_x[:], small_hi[:, 0, :], small_lo[:, 0, :], xh[:], xl[:]).then_inc(S["conv1_done"], 1)
                if not first:
                    pe.wait_ge(S["nm_lo_done"], b)
                passes(bank_y[:], small_hi[:, 1, :], small_lo[:, 1, :], xh[:], xl[:]).then_inc(S["se_done"], 1)
                if first:
                    pe.wait_ge(S["gru_lo_done"], 1)
                else:
                    pe.wait_ge(S["ghn_done"], b)
                gate(bank_v[:], 2, 0, xh[:], xl[:], True, True).then_inc(S["ghn_mm"], 1)
                if not first:
                    pe.wait_ge(S["msgv_done"], b)
                for k in range(T):
                    tile = slice(k * 128, (k + 1) * 128)
                    ins = passes(bank_w[:, tile], xh[:, tile], xl[:, tile], small_hi[:, 2, :], small_lo[:, 2, :])
                ins.then_inc(S["msg_mm"], 1)
                if front:
                    if not first:
                        pe.wait_ge(S["npre_done"], b)
                    front_support(n)
                pe.wait_ge(S["hlo_done"], b + 1)
                conv_part(b, 1, 0)
                conv_part(b, 1, 1)
                pe.wait_ge(S["dadb_done"], b + 1)
                if not first:
                    pe.wait_ge(S["tr_done"], b)
                dist(b, 0)
                if not first:
                    pe.wait_ge(S["tz_done"], b)
                dist(b, 1)
                if front:
                    pe.wait_ge(S["h_done"], b + 1)
                    front_rows(n)
                conv_part(b, 1, 2)
                conv_part(b, 2, 0)
                for k in (2, 3):
                    pe.wait_ge(S["exp_done"], at(b, T, k - 1))
                    dist(b, k)
                if not first:
                    pe.wait_ge(S["msgv_done"], b + 1)
                    tail_rows(t)
                conv_part(b, 2, 1)
                conv_part(b, 2, 2)
                if not front:
                    pe.wait_ge(S["npre_done"], b)
                pe.wait_ge(S["slo_done"], b + 1)
                conv_part(b, 0, 0)
                conv_part(b, 0, 1)
                conv_part(b, 0, 2).then_inc(S["conv2_done"], 1)
                pe.wait_ge(S["q_done"], b + 1)
                pe.wait_ge(S["msglo_done"], b + 1)
                for k in range(T):
                    pe.wait_ge(S["amlo_done"], at(b, T, k + 1))
                    ins = passes(bank_y[:], msg_hi[:, k, :], msg_lo[:, k, :], am_hi[:, k, :], am_lo[:, k, :],
                                 start=k == 0, stop=k == T - 1)
                ins.then_inc(S["nmp_mm"], 1)
                if front:
                    front_x1t(n, 1 - par)
                pe.wait_ge(S["exp_done"], at(b, T, 4))
                gate(bank_a[0][:], 0, 0, xh[:], xl[:], True, False)
                gate(bank_a[1][:], 1, 0, xh[:], xl[:], True, False)
                pe.wait_ge(S["cv_done"], b + 1)
                pe.wait_ge(S["xc_lo_done"], b + 1)
                gate(bank_a[0][:], 0, 1, xc_hi[:], xc_lo[:], False, False)
                gate(bank_p[:], 2, 1, xc_hi[:], xc_lo[:], True, False)
                gate(bank_a[1][:], 1, 1, xc_hi[:], xc_lo[:], False, False)
                pe.wait_ge(S["nm_lo_done"], b + 1)
                gate(bank_a[0][:], 0, 2, nm_hi[:], nm_lo[:], False, True).then_inc(S["r_mm"], 1)
                gate(bank_p[:], 2, 2, nm_hi[:], nm_lo[:], False, True).then_inc(S["n_mm"], 1)
                gate(bank_a[1][:], 1, 2, nm_hi[:], nm_lo[:], False, True).then_inc(S["z_mm"], 1)

            front_support(0)
            pe.wait_ge(S["prep_ident"], 16)
            front_rows(0)
            front_x1t(0, 0)
            pe.wait_ge(S["small_lo_done"], 1)
            pe.wait_ge(S["conv_lo_done"], 1)
            pe.wait_ge(S["pad_done"], 3)
            step(0, 0, first=True)
            with pe.Fori(1, B - 1, 2) as b:
                step(b, 1)
                step(b + 1, 0)
            step(B - 1, 1, front=False)
            tail_rows(B - 1)


def kernel(**inputs):
    import numpy as _np
    import concourse.bacc as _bacc
    from concourse import mybir as _mybir
    from concourse.bass_utils import run_bass_kernel_spmd as _run

    g = {k.removeprefix("L1_gnn_"): _np.asarray(v) for k, v in inputs.items()}
    se = _np.zeros((D, 128), _np.float32)
    b_se = _np.zeros(128, _np.float32)
    for group in range(4):
        for kind in range(3):
            at = 32 * group + SE * kind
            se[:, at:at + SE] = g["w_se"].T
            b_se[at:at + SE] = g["b_se"]
    gates = [g["w_hh"].T, g["w_ih"].T[0:D], g["w_ih"].T[D:2 * D]]
    arrays = {
        "x": g["x"],
        "adj_t": g["adj"].transpose(0, 2, 1),
        "w_conv2": g["conv2_w"].transpose(1, 2, 0),
        "w_gru": _np.stack([w[:, D * k:D * (k + 1)] for w in gates for k in range(3)], axis=1),
        "w_small": _np.stack([g["conv1_w"][:, :, 0].T, se, g["w_msg"].T], axis=1),
        "vectors": _np.stack([g["bn1_g"], g["bn1_b"], g["bn1_m"], g["bn1_v"], g["bn2_g"], g["bn2_b"], g["bn2_m"],
                              g["bn2_v"], *g["b_ih"].reshape(3, D), *g["b_hh"].reshape(3, D), b_se], axis=1),
        "b_msg": g["b_msg"],
        "rows_const": distance_rows(),
        "ident_in": _np.eye(128, dtype=_np.float32),
    }
    arrays = {k: _np.ascontiguousarray(v) for k, v in arrays.items()}
    nc = _bacc.Bacc("TRN2", target_bir_lowering=False, num_devices=1)
    args = [nc.dram_tensor(f"in_{k}", a.shape, _mybir.dt.from_np(a.dtype), kind="ExternalInput").ap()
            for k, a in arrays.items()]
    args.append(nc.dram_tensor("out_0", (B, N, D), _mybir.dt.float32, kind="ExternalOutput").ap())
    build(nc, *args)
    r = _run(nc, [{f"in_{k}": a for k, a in arrays.items()}], core_ids=[0])
    return r.results[0]["out_0"]
```

```python
from contextlib import ExitStack

import numpy as np

import concourse.bass as bass
from concourse import mybir

F32 = mybir.dt.float32
F32R = mybir.dt.float32r
ALU = mybir.AluOpType
ACT = mybir.ActivationFunctionType
AX = mybir.AxisListType

B, N, D = 16, 512, 128
T = N // 128
SE = 3
TAPS = 17
PAD = TAPS // 2
HT = (TAPS + 1) // 2
HALF = N // 2
COMMON = HALF + 2
HW = HT - 2 + COMMON
EPS = 1e-5
MIN_NORM = 1e-15
MAX_NORM = 1.0 - 0.004
ARTANH_MAX = float(np.float32(1 - 1e-07))
WAVES = [0, 1, 4, B]
AHEAD = 4
AHEAD_SUMS = [(3, 4, 8, 8, 8), (0, 5, 12, 0, 0)]
AHEAD_ROOTS = [(0, 14), (14, 28), (28, 48)]
WARM_UP = (6, 10, 2)
SERIES_BELOW = 0.25
SERIES = [1.0 / (2 * k + 1) for k in range(8)]

WHOLE = (0, T, 1)
PARTS = [(0, T // 2, 1), (T // 2, T, 2)]

(V_G1, V_B1, V_M1, V_V1, V_G2, V_B2, V_M2, V_V2, V_IR, V_IZ, V_IN, V_HR, V_HZ, V_HN, V_SE) = range(15)
N_VEC = 15
(C_MU, C_NU, C_AA, C_BA, C_CA, C_AB, C_BB, C_CB) = range(8)
(W_SC1, W_BI1, W_SC2, W_BI2, W_HR, W_HZ, W_HHN, W_NU) = range(8)
W_VE, W_RSTD = 8, 10
N_DER = 12


def distance_rows():
    c = np.zeros((128, 8), np.float32)
    for p in range(128):
        group, row = p // 32, p % 32
        kind = row // SE if row < 3 * SE else 3
        low_a, low_b = group >= 2, group % 2 == 1
        c[p, C_MU] = kind in (1, 2)
        c[p, C_NU] = kind not in (1, 2)
        c[p, C_AA] = kind != 1
        c[p, C_BA] = -0.25 if kind == 1 else 0.0
        c[p, C_CA] = -1.0 if low_a and kind != 1 else 0.0
        c[p, C_AB] = kind != 2
        c[p, C_BB] = -0.25 if kind == 2 else 0.0
        c[p, C_CB] = -1.0 if low_b and kind != 2 else 0.0
    return c


def build(nc, x, adj_t, w_conv2, w_gru, w_small, vectors, b_msg, rows_const, ident_in, out):
    with ExitStack() as ctx:
        def sem(name):
            return ctx.enter_context(nc.semaphore(name))

        def sb(name, shape, dt=F32, where=ctx):
            return where.enter_context(nc.sbuf_tensor(name, shape, dt))

        def psum(name):
            return ctx.enter_context(nc.psum_tensor(name, [128, 512], F32))

        bank_a = [psum("bank_a0"), psum("bank_a1")]
        bank_c = psum("bank_c")
        bank_p = psum("bank_p")
        bank_x = psum("bank_x")
        bank_y = psum("bank_y")
        bank_w = psum("bank_w")
        bank_v = psum("bank_v")

        adj_sb = [sb(f"adj_sb{i}", [128, T, N]) for i in range(2)]
        conv_hi = sb("conv_hi", [128, 3, HT, 128], F32R)
        conv_lo = sb("conv_lo", [128, 3, HT, 128], F32R)
        gru_hi = sb("gru_hi", [128, 9, 128], F32R)
        gru_lo = sb("gru_lo", [128, 9, 128], F32R)
        small_hi = sb("small_hi", [128, 3, 128], F32R)
        small_lo = sb("small_lo", [128, 3, 128], F32R)
        ident = sb("ident", [128, 128])
        vec = sb("vec", [128, N_VEC])
        rows = sb("rows", [128, 8])
        der = sb("der", [128, N_DER])
        bmsg = sb("bmsg", [128, T, 128])
        neg_half_pow = sb("neg_half_pow", [128, T])
        art = sb("art", [128, (B + 1) * T])
        x_rows = [sb(f"x_rows{i}", [128, T, 128]) for i in range(2)]
        xt = sb("xt", [128, T, 128])
        supp = sb("supp", [128, N])
        supp_sq = sb("supp_sq", [128, T, 128])
        ss = sb("ss", [128, T])
        norm0 = sb("norm0", [128, T])
        norm = sb("norm", [128, T])
        rnorm = sb("rnorm", [128, T])
        th = sb("th", [128, T])
        fac = sb("fac", [128, T])
        y1 = sb("y1", [128, T, 128])
        st1 = sb("st1", [128, T, 6])
        mv1 = sb("mv1", [128, 3, T])
        ve1 = sb("ve1", [128, T])
        rstd1 = sb("rstd1", [128, T])
        x1_rows = [sb(f"x1_rows{i}", [128, T, 128]) for i in range(2)]
        x1t = [sb(f"x1t{i}", [128, N]) for i in range(2)]
        x1t_hi = [sb(f"x1t_hi{i}", [128, N], F32R) for i in range(2)]
        x1t_lo = [sb(f"x1t_lo{i}", [128, N], F32R) for i in range(2)]
        h = sb("h", [128, 3, HW])
        h_hi = sb("h_hi", [128, 3, HW], F32R)
        h_lo = sb("h_lo", [128, 3, HW], F32R)
        x1_bias = sb("x1_bias", [128, N])

        sum_sq, root, clipped, inside, recip, log_arg, log, series, small_n = [
            sb(name, [128, B * T]) for name in
            "sum_sq root clipped inside recip log_arg log series small_n".split()]
        pow_half = sb("pow_half", [128, B * T])
        x_ahead = [sb(f"x_ahead{c}", [128, AHEAD * T, 128]) for c in range(2)]
        zeros = sb("zeros", [128, N])
        table_in = sb("table_in", [128, 1])
        nbias1 = sb("nbias1", [128, T])
        nbias2 = sb("nbias2", [128, T])
        prep = ExitStack()
        x_sq = [sb(f"x_sq{i}", [128, T, 128], where=prep) for i in range(2)]
        x_early = [sb(f"x_early{i}", [128, T, 128], where=prep) for i in range(2)]
        w2_st = sb("w2_st", [128, TAPS, 128], where=prep)
        filt = sb("filt", [128, 2, HT, 128], where=prep)
        gru_st = sb("gru_st", [128, 9, 128], where=prep)
        small_st = sb("small_st", [128, 3, 128], where=prep)
        prep.close()

        e = sb("e", [128, T, N])
        am_hi = sb("am_hi", [128, T, N], F32R)
        am_lo = sb("am_lo", [128, T, N], F32R)
        msg = sb("msg", [128, T, 128])
        msg_hi = sb("msg_hi", [128, T, 128], F32R)
        msg_lo = sb("msg_lo", [128, T, 128], F32R)
        s_mix = sb("s_mix", [128, N])
        q = sb("q", [128, N])
        q_hi = sb("q_hi", [128, N], F32R)
        ta = sb("ta", [128, N])
        tb = sb("tb", [128, N])
        da = sb("da", [128, N], F32R)
        db = sb("db", [128, N], F32R)
        cz = sb("cz", [128, N])
        cv = sb("cv", [128, N])
        xc_hi = sb("xc_hi", [128, N], F32R)
        xc_lo = sb("xc_lo", [128, N], F32R)
        nm_hi = sb("nm_hi", [128, N], F32R)
        nm_lo = sb("nm_lo", [128, N], F32R)
        tr = sb("tr", [128, N])
        tz = sb("tz", [128, N])
        ghn = sb("ghn", [128, N])
        un = sb("un", [128, N])
        nn = sb("nn", [128, N])
        xd = sb("xd", [128, N])
        o = sb("o", [128, N])
        y2 = sb("y2", [128, T, 128])
        st2 = sb("st2", [128, T, 6])
        mv2 = sb("mv2", [128, 3, T])
        ve2 = sb("ve2", [128, T])
        rstd2 = sb("rstd2", [128, T])
        y_out = [sb(f"y_out{i}", [128, T, 128]) for i in range(2)]

        names = """x_early0 x_early1 x_ahead0 x_ahead1 prep_rows prep_ident prep_bmsg prep_w2 prep_gru prep_small prep_vec adj_in0 adj_in1
            x_in0 x_in1 stored0 stored1
            sum_sq_done small_step root_done ln_done ln_ready art_done pool_const pad_done zeros_done
            vec_eps vec_pow vec_done filt_done conv_hi_done gru_hi_done small_lo_done conv_lo_done gru_lo_done
            xt_done pow_ns pow_v1 pow_v2 xd_done
            conv1_done se_done msg_mm ghn_mm conv2_done dist_mm supp_mm srow_mm out_mm nmp_mm
            r_mm z_mm n_mm x1t_mm
            tr_done tz_done h_done smix_done small_hi_done nn_done msg_hi_done ghn_done tatb_done exp_done
            supp_out ss_done th_done xc_hi_done nm_hi_done x1t_out
            un_done npre_done hhi_done hlo_done hsum_done shi_done slo_done q_done qhi_done da_done dadb_done
            msgv_done msglo_done gate_done o_done am_done amhi_done amlo_done norm_done rnorm_done fac_done
            y1_done st1_done mv1_done ve1_done x1_done cz_done cv_done xc_lo_done
            y2_done st2_done mv2_done ve2_done nb1_done nb2_done out_done nm_lo_done x1t_lo_done""".split()
        S = {n: sem(n) for n in names}

        def at(b, per, k):
            return b * per + k

        def columns(part):
            return slice(part[0] * 128, part[1] * 128)

        xr_dram = x.rearrange("b (t p) d -> b p t d", p=128)
        adj_dram = adj_t.rearrange("b (t p) i -> b p t i", p=128)
        out_dram = out.rearrange("b (t p) d -> b p t d", p=128)

        def row_of(dram, b):
            return dram[b] if isinstance(b, int) else dram[bass.ds(b, 1)].rearrange("a p t d -> (a p) t d")

        block = ctx.enter_context(nc.Block())

        @block.sync
        def _(sp):
            def load_x(b, par):
                sp.dma_start(x_rows[par][:], row_of(xr_dram, b)).then_inc(S[f"x_in{par}"], 16)

            def load_adj(b, par):
                sp.dma_start(adj_sb[par][:], row_of(adj_dram, b)).then_inc(S[f"adj_in{par}"], 16)

            def load(n, par):
                sp.wait_ge(S["y1_done"], at(n - 2, T, T))
                load_x(n, par)
                sp.wait_ge(S["am_done"], at(n - 2, T, T))
                load_adj(n, par)

            def load_ahead(c):
                b0 = WAVES[2] + AHEAD * c
                sp.dma_start(x_ahead[c % 2][:], x[b0:b0 + AHEAD].rearrange("b (t p) d -> p (b t) d", p=128)
                             ).then_inc(S[f"x_ahead{c % 2}"], 16)

            def store(b, par):
                sp.wait_ge(S["out_done"], at(b, T, T))
                sp.dma_start(row_of(out_dram, b), y_out[par][:]).then_inc(S[f"stored{par}"], 16)

            def store_part(b, par, part):
                sp.wait_ge(S["out_done"], at(b, T, part[1]))
                tiles = slice(part[0], part[1])
                sp.dma_start(row_of(out_dram, b)[:, tiles, :], y_out[par][:, tiles, :]).then_inc(S[f"stored{par}"], 16)

            load_x(0, 0)
            sp.dma_start(vec[:], vectors).then_inc(S["prep_vec"], 16)
            sp.dma_start(rows[:], rows_const).then_inc(S["prep_rows"], 16)
            load_adj(0, 0)
            load_x(1, 1)
            for i in range(2):
                sp.dma_start(x_early[i][:], row_of(xr_dram, 2 + i)).then_inc(S[f"x_early{i}"], 16)
            sp.dma_start(w2_st[:], w_conv2).then_inc(S["prep_w2"], 16)
            sp.dma_start(small_st[:], w_small).then_inc(S["prep_small"], 16)
            sp.dma_start(ident[:], ident_in).then_inc(S["prep_ident"], 16)
            sp.dma_start(gru_st[:], w_gru).then_inc(S["prep_gru"], 16)
            sp.dma_start(bmsg[:], b_msg.rearrange("(a c d) -> a c d", a=1, c=1).to_broadcast([128, T, 128])
                         ).then_inc(S["prep_bmsg"], 16)
            load_adj(1, 1)
            load_ahead(0)
            load_ahead(1)
            sp.wait_ge(S["sum_sq_done"], (WAVES[2] + AHEAD) * T)
            load_ahead(2)
            load(2, 0)
            with sp.Fori(3, B - 1, 2) as n:
                load(n, 1)
                store(n - 3, 0)
                load(n + 1, 0)
                store(n - 2, 1)
            load(B - 1, 1)
            for b in range(B - 4, B - 1):
                store(b, b % 2)
            for part in PARTS:
                store_part(B - 1, 1, part)
            sp.wait_ge(S["stored0"], 16 * (B // 2))
            sp.wait_ge(S["stored1"], 16 * (B // 2 + 1))

        @block.gpsimd
        def _(pool):
            pool.memset(pow_half[:], 0.5).then_inc(S["pool_const"], 1)
            pool.memset(neg_half_pow[:], -0.5).then_inc(S["pool_const"], 1)
            pool.wait_ge(S["pool_const"], 2)
            pool.wait_ge(S["vec_eps"], 2)
            pool.tensor_tensor(der[:, W_RSTD:W_RSTD + 2], der[:, W_VE:W_VE + 2], neg_half_pow[:, 0:2], ALU.pow
                               ).then_inc(S["vec_pow"], 1)

            def roots(k0, k1):
                pool.wait_ge(S["sum_sq_done"], k1)
                pool.tensor_tensor(root[:, k0:k1], sum_sq[:, k0:k1], pow_half[:, k0:k1], ALU.pow
                                   ).then_inc(S["root_done"], 1)

            def roots_ahead(part):
                roots(WAVES[2] * T + AHEAD_ROOTS[part][0], WAVES[2] * T + AHEAD_ROOTS[part][1])

            def front_xt(n, par, loaded):
                pool.wait_ge(S[f"x_in{par}"], loaded)
                if isinstance(n, int):
                    pool.wait_ge(S["art_done"], 1 + (n >= WAVES[1]) + (n >= WAVES[2]))
                if not (isinstance(n, int) and n == 0):
                    pool.wait_ge(S["supp_mm"], n)
                a = art[:, n * T:(n + 1) * T] if isinstance(n, int) else art[:, bass.ds(n * T, T)]
                pool.tensor_tensor(xt[:], x_rows[par][:], a.unsqueeze(2).to_broadcast([128, T, 128]), ALU.mult
                                   ).then_inc(S["xt_done"], 1)

            def main_hsum(b):
                pool.wait_ge(S["h_done"], b + 1)
                pool.tensor_tensor(h[:, 2, :], h[:, 0, :], h[:, 1, :], ALU.add).then_inc(S["hsum_done"], 1)
                pool.tensor_tensor(h_hi[:, 2, :], h[:, 0, :], h[:, 1, :], ALU.add).then_inc(S["shi_done"], 1)
                pool.wait_ge(S["hsum_done"], b + 1)
                pool.wait_ge(S["shi_done"], b + 1)
                pool.tensor_tensor(h_lo[:, 2, :], h[:, 2, :], h_hi[:, 2, :].bitcast(F32), ALU.subtract
                                   ).then_inc(S["slo_done"], 1)

            def front_pow_norm(n):
                pool.wait_ge(S["ss_done"], at(n, T, T))
                pool.tensor_tensor(norm0[:], ss[:], pow_half[:, 0:T], ALU.pow).then_inc(S["pow_ns"], 1)

            def front_pow_rstd(n):
                pool.wait_ge(S["ve1_done"], n + 1)
                pool.tensor_tensor(rstd1[:], ve1[:], neg_half_pow[:], ALU.pow).then_inc(S["pow_v1"], 1)

            def tail_xd(t, par):
                pool.wait_ge(S["nn_done"], t + 1)
                pool.tensor_tensor(xd[:], x1t[par][:], nn[:], ALU.subtract).then_inc(S["xd_done"], 1)

            def tail_pow(t, part=WHOLE):
                a, z, number = part
                pool.wait_ge(S["ve2_done"], at(t, 1, number))
                pool.tensor_tensor(rstd2[:, a:z], ve2[:, a:z], neg_half_pow[:, a:z], ALU.pow).then_inc(S["pow_v2"], 1)

            def step(b, par, first=False, front=True, loaded=None, early=None, late=None):
                n, t = b + 1, b - 1
                if front:
                    front_xt(n, 1 - par, loaded)
                if not first:
                    tail_xd(t, 1 - par)
                main_hsum(b)
                if early is not None:
                    roots_ahead(early)
                if front:
                    front_pow_norm(n)
                    front_pow_rstd(n)
                if late is not None:
                    roots_ahead(late)
                if not first:
                    tail_pow(t)

            roots(0, WAVES[1] * T)
            front_xt(0, 0, 16)
            roots(WAVES[1] * T, WAVES[2] * T)
            front_pow_norm(0)
            front_pow_rstd(0)
            step(0, 0, first=True, loaded=16, late=0)
            step(1, 1, loaded=32, early=1, late=2)
            step(2, 0, loaded=32)
            with pool.Fori(3, B - 1, 2) as b:
                step(b, 1, loaded=8 * b + 24)
                step(b + 1, 0, loaded=8 * b + 24)
            step(B - 1, 1, front=False)
            for part in PARTS:
                tail_pow(B - 1, part)

        @block.scalar
        def _(act):
            def sum_squares(dst, src, b0, tiles):
                for k in tiles:
                    act.activation(dst[:, k, :], src[:, k, :], ACT.Square, accum_out=sum_sq[:, b0 * T + k:b0 * T + k + 1]
                                   ).then_inc(S["sum_sq_done"], 1)

            def squares_ahead(step, point):
                k0 = sum(sum(counts) for counts in AHEAD_SUMS[:step]) + sum(AHEAD_SUMS[step][:point])
                for k in range(k0, k0 + AHEAD_SUMS[step][point]):
                    c, k_in = divmod(k, AHEAD * T)
                    if k_in == 0:
                        act.wait_ge(S[f"x_ahead{c % 2}"], 16 * (c // 2 + 1))
                    sum_squares(x_ahead[c % 2], x_ahead[c % 2], WAVES[2] + AHEAD * c, (k_in,))

            def logs(wave):
                act.wait_ge(S["ln_ready"], wave + 1)
                c = slice(WAVES[wave] * T, WAVES[wave + 1] * T)
                act.activation(log[:, c], log_arg[:, c], ACT.Ln).then_inc(S["ln_done"], 1)

            def filter_high(k):
                act.wait_ge(S["filt_done"], k + 1)
                act.activation(conv_hi[:, 1 + k, :, :], filt[:, k, :, :], ACT.Copy).then_inc(S["conv_hi_done"], 1)

            def tanh_table():
                act.activation(table_in[:], pow_half[:, 0:1], ACT.Tanh)

            def front_support(n):
                act.wait_ge(S["supp_mm"], n + 1)
                act.activation(supp[:], bank_p[:], ACT.Copy).then_inc(S["supp_out"], 1)

            def front_squares(n):
                act.wait_ge(S["srow_mm"], n + 1)
                for t in range(T):
                    act.activation(supp_sq[:, t, :], bank_x[:, t * 128:(t + 1) * 128], ACT.Square,
                                   accum_out=ss[:, t:t + 1]).then_inc(S["ss_done"], 1)

            def front_tanh(n):
                act.wait_ge(S["norm_done"], n + 1)
                act.activation(th[:], norm[:], ACT.Tanh).then_inc(S["th_done"], 1)

            def front_x1(n, par):
                if not (isinstance(n, int) and n < 2):
                    act.wait_ge(S["y2_done"], n - 1)
                act.wait_ge(S["nb1_done"], n + 1)
                for t in range(T):
                    act.activation(x1_rows[par][:, t, :], y1[:, t, :], ACT.Identity, bias=nbias1[:, t:t + 1],
                                   scale=rstd1[:, t:t + 1]).then_inc(S["x1_done"], 1)

            def front_x1t(n, par):
                act.wait_ge(S["x1t_mm"], n + 1)
                act.activation(x1t_hi[par][:], bank_x[:], ACT.Copy)
                act.activation(x1t[par][:], bank_x[:], ACT.Copy).then_inc(S["x1t_out"], 1)
                act.activation(x1_bias[:], bank_x[:], ACT.Identity, bias=der[:, W_BI2:W_BI2 + 1]
                               ).then_inc(S["x1t_out"], 1)

            def tail_r(t, part=WHOLE):
                act.wait_ge(S["r_mm"], t + 1)
                act.activation(tr[:, columns(part)], bank_a[0][:, columns(part)], ACT.Tanh, bias=der[:, W_HR:W_HR + 1],
                               scale=0.5).then_inc(S["tr_done"], 1)

            def tail_z(t, part=WHOLE):
                act.wait_ge(S["z_mm"], t + 1)
                act.activation(tz[:, columns(part)], bank_a[1][:, columns(part)], ACT.Tanh, bias=der[:, W_HZ:W_HZ + 1],
                               scale=0.5).then_inc(S["tz_done"], 1)

            def tail_n(t, part=WHOLE):
                act.wait_ge(S["npre_done"], at(t, 1, part[2]))
                act.activation(nn[:, columns(part)], un[:, columns(part)], ACT.Tanh, bias=vec[:, V_IN:V_IN + 1]
                               ).then_inc(S["nn_done"], 1)

            def main_h(b):
                act.wait_ge(S["conv1_done"], b + 1)
                for buf, done in ((h, "h_done"), (h_hi, "hhi_done")):
                    act.activation(buf[:, 0:2, PAD // 2:PAD // 2 + HALF], bank_x[:].rearrange("p (m g) -> p g m", g=2),
                                   ACT.Relu, bias=der[:, W_BI1:W_BI1 + 1], scale=der[:, W_SC1:W_SC1 + 1]
                                   ).then_inc(S[done], 1)

            def main_mix(b):
                act.wait_ge(S["se_done"], b + 1)
                act.activation(s_mix[:], bank_y[:], ACT.Identity, bias=der[:, W_NU:W_NU + 1],
                               scale=rows[:, C_MU:C_MU + 1]).then_inc(S["smix_done"], 1)

            def main_ghn(b):
                act.wait_ge(S["ghn_mm"], b + 1)
                act.activation(ghn[:], bank_v[:], ACT.Identity, bias=der[:, W_HHN:W_HHN + 1], scale=0.5
                               ).then_inc(S["ghn_done"], 1)

            def main_msg(b):
                act.wait_ge(S["msgv_done"], b + 1)
                act.activation(msg_hi[:], msg[:], ACT.Relu).then_inc(S["msg_hi_done"], 1)

            def main_tab(b):
                act.wait_ge(S["q_done"], b + 1)
                act.activation(q_hi[:], q[:], ACT.Copy).then_inc(S["qhi_done"], 1)
                act.activation(ta[:], q[:], ACT.Identity, bias=rows[:, C_BA:C_BA + 1], scale=rows[:, C_AA:C_AA + 1]
                               ).then_inc(S["tatb_done"], 1)
                act.activation(tb[:], q[:], ACT.Identity, bias=rows[:, C_BB:C_BB + 1], scale=rows[:, C_AB:C_AB + 1]
                               ).then_inc(S["tatb_done"], 1)

            def main_exp(b, t):
                act.wait_ge(S["dist_mm"], at(b, T, t + 1))
                act.activation(e[:, t, :], bank_a[t % 2][:], ACT.Exp, scale=2.0).then_inc(S["exp_done"], 1)

            def main_amhi(b, t):
                act.wait_ge(S["am_done"], at(b, T, t + 1))
                act.activation(am_hi[:, t, :], e[:, t, :], ACT.Copy).then_inc(S["amhi_done"], 1)

            def main_conv_hi(b):
                act.wait_ge(S["cv_done"], b + 1)
                act.activation(xc_hi[:], cv[:], ACT.Relu).then_inc(S["xc_hi_done"], 1)

            def main_nm_hi(b):
                act.wait_ge(S["nmp_mm"], b + 1)
                act.activation(nm_hi[:], bank_y[:], ACT.Copy).then_inc(S["nm_hi_done"], 1)

            def tail_out(t, par, stored, part=WHOLE):
                act.wait_ge(S["nb2_done"], at(t, 1, part[2]))
                if stored is not None:
                    act.wait_ge(S[f"stored{par}"], stored)
                for k in range(part[0], part[1]):
                    act.activation(y_out[par][:, k, :], y2[:, k, :], ACT.Identity, bias=nbias2[:, k:k + 1],
                                   scale=rstd2[:, k:k + 1]).then_inc(S["out_done"], 1)

            def step(b, par, front=True, stored=None):
                n, t = b + 1, b - 1
                early = isinstance(b, int) and b < len(AHEAD_SUMS)
                with_logs = isinstance(b, int) and b == len(AHEAD_SUMS)
                if not (isinstance(b, int) and b < 1):
                    tail_r(t)
                    tail_z(t)
                main_h(b)
                main_mix(b)
                if not (isinstance(b, int) and b < 1):
                    tail_n(t)
                if early:
                    squares_ahead(b, 0)
                main_tab(b)
                main_msg(b)
                if front:
                    front_support(n)
                if not (isinstance(b, int) and b < 2):
                    tail_out(b - 2, par, stored)
                if early:
                    squares_ahead(b, 1)
                main_exp(b, 0)
                main_exp(b, 1)
                if front:
                    front_squares(n)
                main_amhi(b, 0)
                main_amhi(b, 1)
                main_exp(b, 2)
                main_exp(b, 3)
                if front:
                    front_tanh(n)
                if early:
                    squares_ahead(b, 2)
                main_amhi(b, 2)
                main_amhi(b, 3)
                if early:
                    squares_ahead(b, 3)
                if with_logs:
                    logs(2)
                    tanh_table()
                if front:
                    front_x1(n, 1 - par)
                main_conv_hi(b)
                main_nm_hi(b)
                if front:
                    front_x1t(n, 1 - par)
                main_ghn(b)
                if early:
                    squares_ahead(b, 4)

            act.wait_ge(S["x_in0"], 16)
            sum_squares(x_sq[0], x_rows[0], 0, range(T))
            logs(0)
            tanh_table()
            act.wait_ge(S["x_in1"], 16)
            sum_squares(x_sq[1], x_rows[1], 1, range(T))
            for i in range(2):
                act.wait_ge(S[f"x_early{i}"], 16)
                sum_squares(x_early[i], x_early[i], 2 + i, range(T))
            act.wait_ge(S["prep_small"], 16)
            act.activation(small_hi[:], small_st[:], ACT.Copy).then_inc(S["small_hi_done"], 1)
            front_support(0)
            front_squares(0)
            filter_high(0)
            front_tanh(0)
            logs(1)
            tanh_table()
            filter_high(1)
            act.wait_ge(S["prep_w2"], 16)
            act.activation(conv_hi[:, 0, 0:HT - 1, :], w2_st[:, 1:TAPS:2, :], ACT.Copy).then_inc(S["conv_hi_done"], 1)
            front_x1(0, 0)
            act.wait_ge(S["vec_done"], 1)
            front_x1t(0, 0)
            act.wait_ge(S["prep_gru"], 16)
            act.activation(gru_hi[:], gru_st[:], ACT.Copy).then_inc(S["gru_hi_done"], 1)
            step(0, 0)
            step(1, 1)
            step(2, 0)
            step(3, 1)
            step(4, 0, stored=16)
            with act.Fori(5, B - 1, 2) as b:
                step(b, 1, stored=8 * b - 24)
                step(b + 1, 0, stored=8 * b - 8)
            step(B - 1, 1, front=False, stored=8 * (B - 1) - 24)
            for part in PARTS:
                tail_r(B - 1, part)
            for part in PARTS:
                tail_n(B - 1, part)
                tail_z(B - 1, part)
            tail_out(B - 2, 0, 8 * (B - 1) - 8)
            for part in PARTS:
                tail_out(B - 1, 1, 8 * (B + 1) - 24, part)

        @block.vector
        def _(dve):
            steps = [0]

            def small(ins):
                steps[0] += 1
                ins.then_inc(S["small_step"], 1)
                dve.wait_ge(S["small_step"], steps[0])

            dve.memset(zeros[:], 0.0).then_inc(S["zeros_done"], 1)
            for buf in (h, h_hi, h_lo):
                v = buf[:] if buf is h else buf[:].bitcast(F32)
                dve.memset(v[:, :, 0:PAD // 2], 0.0)
                dve.memset(v[:, :, PAD // 2 + HALF:HW], 0.0).then_inc(S["pad_done"], 1)

            dve.wait_ge(S["prep_vec"], 16)
            dve.wait_ge(S["prep_rows"], 16)
            dve.tensor_scalar(der[:, W_VE:W_VE + 1], vec[:, V_V1:V_V1 + 1], EPS, None, ALU.add).then_inc(S["vec_eps"], 1)
            dve.tensor_scalar(der[:, W_VE + 1:W_VE + 2], vec[:, V_V2:V_V2 + 1], EPS, None, ALU.add).then_inc(S["vec_eps"], 1)

            def series_of(wave):
                c = slice(WAVES[wave] * T, WAVES[wave + 1] * T)
                dve.wait_ge(S["sum_sq_done"], WAVES[wave + 1] * T)
                small(dve.tensor_scalar(inside[:, c], sum_sq[:, c], 1.0, None, ALU.min))
                small(dve.tensor_scalar(series[:, c], inside[:, c], SERIES[-1], None, ALU.mult))
                for k in SERIES[-2:0:-1]:
                    small(dve.scalar_tensor_tensor(series[:, c], series[:, c], k, inside[:, c], ALU.add, ALU.mult))
                small(dve.tensor_scalar(series[:, c], series[:, c], SERIES[0], None, ALU.add))

            def log_in(wave, roots):
                c = slice(WAVES[wave] * T, WAVES[wave + 1] * T)
                dve.wait_ge(S["root_done"], roots)
                small(dve.tensor_scalar(clipped[:, c], root[:, c], MIN_NORM, None, ALU.max))
                small(dve.tensor_scalar(inside[:, c], clipped[:, c], ARTANH_MAX, None, ALU.min))
                small(dve.tensor_scalar(recip[:, c], inside[:, c], -1.0, 1.0, ALU.mult, ALU.add))
                small(dve.reciprocal(recip[:, c], recip[:, c]))
                dve.scalar_tensor_tensor(log_arg[:, c], inside[:, c], 1.0, recip[:, c], ALU.add, ALU.mult
                                         ).then_inc(S["ln_ready"], 1)
                dve.tensor_scalar(small_n[:, c], inside[:, c], SERIES_BELOW, None, ALU.is_lt)
                small(dve.reciprocal(clipped[:, c], clipped[:, c]))

            def art_out(wave):
                c = slice(WAVES[wave] * T, WAVES[wave + 1] * T)
                dve.wait_ge(S["ln_done"], wave + 1)
                small(dve.scalar_tensor_tensor(log[:, c], log[:, c], 0.5, clipped[:, c], ALU.mult, ALU.mult))
                small(dve.tensor_tensor(series[:, c], series[:, c], log[:, c], ALU.subtract))
                small(dve.tensor_tensor(series[:, c], series[:, c], small_n[:, c], ALU.mult))
                dve.tensor_tensor(art[:, c], log[:, c], series[:, c], ALU.add).then_inc(S["art_done"], 1)

            def channel_vectors():
                small(dve.tensor_tensor(der[:, W_HR:W_HR + 2], vec[:, V_IR:V_IR + 2], vec[:, V_HR:V_HR + 2], ALU.add))
                small(dve.tensor_scalar(der[:, W_HR:W_HR + 2], der[:, W_HR:W_HR + 2], 0.5, None, ALU.mult))
                small(dve.tensor_scalar(der[:, W_HHN:W_HHN + 1], vec[:, V_HN:V_HN + 1], 0.5, None, ALU.mult))
                small(dve.tensor_tensor(der[:, W_NU:W_NU + 1], vec[:, V_SE:V_SE + 1], rows[:, C_MU:C_MU + 1], ALU.mult))
                small(dve.tensor_tensor(der[:, W_NU:W_NU + 1], der[:, W_NU:W_NU + 1], rows[:, C_NU:C_NU + 1], ALU.add))
                dve.wait_ge(S["vec_pow"], 1)
                for k, (g, bb, m, sc, bi) in enumerate(((V_G1, V_B1, V_M1, W_SC1, W_BI1),
                                                        (V_G2, V_B2, V_M2, W_SC2, W_BI2))):
                    small(dve.tensor_tensor(der[:, sc:sc + 1], vec[:, g:g + 1], der[:, W_RSTD + k:W_RSTD + k + 1], ALU.mult))
                    small(dve.tensor_tensor(der[:, bi:bi + 1], vec[:, m:m + 1], der[:, sc:sc + 1], ALU.mult))
                    ins = dve.tensor_tensor(der[:, bi:bi + 1], vec[:, bb:bb + 1], der[:, bi:bi + 1], ALU.subtract)
                ins.then_inc(S["vec_done"], 1)

            def filters():
                dve.wait_ge(S["prep_w2"], 16)
                even = w2_st[:, 0:TAPS:2, :]
                odd = w2_st[:, 1:TAPS:2, :]
                dve.tensor_tensor(filt[:, 0, 0:HT - 1, :], even[:, 0:HT - 1, :], odd, ALU.subtract)
                dve.tensor_copy(filt[:, 0, HT - 1, :], even[:, HT - 1, :]).then_inc(S["filt_done"], 1)
                dve.tensor_tensor(filt[:, 1, 1:HT, :], even[:, 1:HT, :], odd, ALU.subtract)
                dve.tensor_copy(filt[:, 1, 0, :], even[:, 0, :]).then_inc(S["filt_done"], 1)

            def conv_low(g, part, src):
                dve.wait_ge(S["conv_hi_done"], part)
                taps = src.shape[1]
                dve.tensor_tensor(conv_lo[:, g, 0:taps, :], src, conv_hi[:, g, 0:taps, :].bitcast(F32), ALU.subtract
                                  ).then_inc(S["conv_lo_done"], 1)

            def front_norm(n):
                dve.wait_ge(S["pow_ns"], n + 1)
                dve.tensor_scalar(norm[:], norm0[:], MIN_NORM, None, ALU.max).then_inc(S["norm_done"], 1)

            def front_factor(n):
                dve.wait_ge(S["norm_done"], n + 1)
                dve.reciprocal(rnorm[:], norm[:]).then_inc(S["rnorm_done"], 1)
                dve.wait_ge(S["rnorm_done"], n + 1)
                dve.wait_ge(S["th_done"], n + 1)
                dve.scalar_tensor_tensor(fac[:], th[:], MAX_NORM, rnorm[:], ALU.min, ALU.mult).then_inc(S["fac_done"], 1)

            def front_y1(n, par):
                dve.wait_ge(S["fac_done"], n + 1)
                for t in range(T):
                    dve.scalar_tensor_tensor(y1[:, t, :], bank_x[:, t * 128:(t + 1) * 128], fac[:, t:t + 1],
                                             x_rows[par][:, t, :], ALU.mult, ALU.add).then_inc(S["y1_done"], 1)

            def stats(y, st, mv, ve, b, y_sem, y_per, st_sem, mv_sem, ve_sem, part=WHOLE):
                a, z, number = part
                for t in range(a, z):
                    dve.wait_ge(S[y_sem], at(b, y_per, t + 1 if y_per == T else number))
                    dve.bn_stats(st[:, t, :], y[:, t, :]).then_inc(S[st_sem], 1)
                dve.wait_ge(S[st_sem], at(b, T, z))
                dve.tensor_tensor(mv[:, 0, a:z], st[:, a:z, 1], st[:, a:z, 4], ALU.add)
                dve.tensor_tensor(mv[:, 1, a:z], st[:, a:z, 1], st[:, a:z, 4], ALU.subtract)
                dve.tensor_tensor(mv[:, 2, a:z], st[:, a:z, 2], st[:, a:z, 5], ALU.add).then_inc(S[mv_sem], 1)
                dve.wait_ge(S[mv_sem], at(b, 2, 2 * number - 1))
                dve.tensor_scalar(mv[:, 0, a:z], mv[:, 0, a:z], 0.5, None, ALU.mult)
                dve.scalar_tensor_tensor(mv[:, 1, a:z], mv[:, 1, a:z], 0.25, mv[:, 1, a:z], ALU.mult, ALU.mult)
                dve.tensor_scalar(mv[:, 2, a:z], mv[:, 2, a:z], 1.0 / D, EPS, ALU.mult, ALU.add).then_inc(S[mv_sem], 1)
                dve.wait_ge(S[mv_sem], at(b, 2, 2 * number))
                dve.tensor_tensor(ve[:, a:z], mv[:, 1, a:z], mv[:, 2, a:z], ALU.add).then_inc(S[ve_sem], 1)

            def front_bias(n):
                dve.wait_ge(S["pow_v1"], n + 1)
                dve.scalar_tensor_tensor(nbias1[:], mv1[:, 0, :], -1.0, rstd1[:], ALU.mult, ALU.mult
                                         ).then_inc(S["nb1_done"], 1)

            def front_x1lo(n, par):
                dve.wait_ge(S["x1t_out"], at(n, 2, 1))
                dve.tensor_tensor(x1t_lo[par][:], x1t[par][:], x1t_hi[par][:].bitcast(F32), ALU.subtract
                                  ).then_inc(S["x1t_lo_done"], 1)

            def tail_r(t, part=WHOLE):
                c = columns(part)
                dve.wait_ge(S["tr_done"], at(t, 1, part[2]))
                dve.wait_ge(S["ghn_done"], t + 1)
                dve.scalar_tensor_tensor(un[:, c], tr[:, c], 1.0, ghn[:, c], ALU.add, ALU.mult).then_inc(S["un_done"], 1)

            def tail_n(t, part=WHOLE):
                c = columns(part)
                dve.wait_ge(S["un_done"], at(t, 1, part[2]))
                dve.wait_ge(S["n_mm"], t + 1)
                dve.tensor_tensor(un[:, c], bank_p[:, c], un[:, c], ALU.add).then_inc(S["npre_done"], 1)

            def tail_o(t, part=WHOLE):
                c = columns(part)
                dve.wait_ge(S["xd_done"], at(t, 1, part[2]))
                dve.wait_ge(S["tz_done"], at(t, 1, part[2]))
                dve.scalar_tensor_tensor(xd[:, c], tz[:, c], 1.0, xd[:, c], ALU.add, ALU.mult).then_inc(S["gate_done"], 1)
                dve.wait_ge(S["gate_done"], at(t, 1, part[2]))
                dve.scalar_tensor_tensor(o[:, c], xd[:, c], 0.5, nn[:, c], ALU.mult, ALU.add).then_inc(S["o_done"], 1)

            def tail_y2(t, par, part=WHOLE, bank=bank_w):
                a, z, number = part
                dve.wait_ge(S["out_mm"], at(t, 1, number))
                dve.tensor_tensor(y2[:, a:z, :], bank[:].rearrange("p (t d) -> p t d", t=T)[:, a:z, :],
                                  x1_rows[par][:, a:z, :], ALU.add).then_inc(S["y2_done"], 1)

            def tail_stats(t, part=WHOLE):
                stats(y2, st2, mv2, ve2, t, "y2_done", 1, "st2_done", "mv2_done", "ve2_done", part)

            def tail_bias(t, part=WHOLE):
                a, z, number = part
                dve.wait_ge(S["pow_v2"], at(t, 1, number))
                dve.scalar_tensor_tensor(nbias2[:, a:z], mv2[:, 0, a:z], -1.0, rstd2[:, a:z], ALU.mult, ALU.mult
                                         ).then_inc(S["nb2_done"], 1)

            def main_h(b):
                dve.wait_ge(S["hhi_done"], b + 1)
                dve.tensor_tensor(h_lo[:, 0:2, :], h[:, 0:2, :], h_hi[:, 0:2, :].bitcast(F32), ALU.subtract
                                  ).then_inc(S["hlo_done"], 1)

            def main_q(b):
                dve.wait_ge(S["smix_done"], b + 1)
                dve.scalar_tensor_tensor(q[:], bank_y[:], vec[:, V_SE:V_SE + 1], s_mix[:], ALU.add, ALU.mult
                                         ).then_inc(S["q_done"], 1)

            def main_dab(b):
                dve.wait_ge(S["qhi_done"], b + 1)
                dve.wait_ge(S["tatb_done"], at(b, 2, 2))
                dve.scalar_tensor_tensor(da[:], q_hi[:].bitcast(F32), rows[:, C_CA:C_CA + 1], ta[:], ALU.mult, ALU.add
                                         ).then_inc(S["da_done"], 1)
                dve.scalar_tensor_tensor(db[:], q_hi[:].bitcast(F32), rows[:, C_CB:C_CB + 1], tb[:], ALU.mult, ALU.add
                                         ).then_inc(S["dadb_done"], 1)

            def main_msgv(b):
                if isinstance(b, int) and b == 0:
                    dve.wait_ge(S["prep_bmsg"], 16)
                    dve.wait_ge(S["conv_lo_done"], 3)
                    dve.wait_ge(S["gru_lo_done"], 1)
                dve.wait_ge(S["msg_mm"], b + 1)
                dve.tensor_tensor(msg[:], bank_w[:].rearrange("p (t d) -> p t d", t=T), bmsg[:], ALU.add
                                  ).then_inc(S["msgv_done"], 1)

            def main_msglo(b):
                dve.wait_ge(S["msg_hi_done"], b + 1)
                dve.scalar_tensor_tensor(msg_lo[:], msg[:], 0.0, msg_hi[:].bitcast(F32), ALU.max, ALU.subtract
                                         ).then_inc(S["msglo_done"], 1)

            def main_am(b, par, t):
                dve.wait_ge(S["exp_done"], at(b, T, t + 1))
                dve.tensor_tensor(e[:, t, :], e[:, t, :], adj_sb[par][:, t, :], ALU.mult).then_inc(S["am_done"], 1)

            def main_amlo(b, t):
                dve.wait_ge(S["amhi_done"], at(b, T, t + 1))
                dve.tensor_tensor(am_lo[:, t, :], e[:, t, :], am_hi[:, t, :].bitcast(F32), ALU.subtract
                                  ).then_inc(S["amlo_done"], 1)

            def main_conv(b):
                dve.wait_ge(S["conv2_done"], b + 1)
                dve.wait_ge(S["x1t_out"], at(b, 2, 2))
                xb = x1_bias[:].rearrange("p (m g) -> p g m", g=2)
                zv = cz[:].rearrange("p (g m) -> p g m", g=2)
                for g in range(2):
                    ins = dve.scalar_tensor_tensor(zv[:, g, :], bank_p[:, g:g + HALF], der[:, W_SC2:W_SC2 + 1],
                                                   xb[:, g, :], ALU.mult, ALU.add)
                ins.then_inc(S["cz_done"], 1)
                dve.wait_ge(S["cz_done"], b + 1)
                dve.scalar_tensor_tensor(cv[:].rearrange("p (m g) -> p g m", g=2),
                                         bank_c[:].rearrange("p (g m) -> p g m", g=2), der[:, W_SC2:W_SC2 + 1],
                                         zv, ALU.mult, ALU.add).then_inc(S["cv_done"], 1)

            def main_conv_lo(b):
                dve.wait_ge(S["xc_hi_done"], b + 1)
                dve.scalar_tensor_tensor(xc_lo[:], cv[:], 0.0, xc_hi[:].bitcast(F32), ALU.max, ALU.subtract
                                         ).then_inc(S["xc_lo_done"], 1)

            def main_nm_lo(b):
                dve.wait_ge(S["nm_hi_done"], b + 1)
                dve.tensor_tensor(nm_lo[:], bank_y[:], nm_hi[:].bitcast(F32), ALU.subtract).then_inc(S["nm_lo_done"], 1)

            def step(b, par, first=False, front=True):
                n, t = b + 1, b - 1
                if not first:
                    tail_r(t)
                    tail_n(t)
                main_h(b)
                main_q(b)
                main_msgv(b)
                if not (isinstance(b, int) and b < 2):
                    tail_bias(b - 2)
                if isinstance(b, int) and b == 2:
                    series_of(2)
                main_dab(b)
                if not first:
                    tail_o(t)
                main_msglo(b)
                main_am(b, par, 0)
                main_am(b, par, 1)
                if not first:
                    tail_y2(t, 1 - par)
                main_amlo(b, 0)
                main_amlo(b, 1)
                if front:
                    front_norm(n)
                main_am(b, par, 2)
                if front:
                    front_factor(n)
                    front_y1(n, 1 - par)
                main_am(b, par, 3)
                if front:
                    stats(y1, st1, mv1, ve1, n, "y1_done", T, "st1_done", "mv1_done", "ve1_done")
                main_amlo(b, 2)
                main_amlo(b, 3)
                if front:
                    front_bias(n)
                main_conv(b)
                main_conv_lo(b)
                main_nm_lo(b)
                if front:
                    front_x1lo(n, 1 - par)
                if isinstance(b, int) and b == 2:
                    art_out(2)
                if not first:
                    tail_stats(t)
                if isinstance(b, int) and b == 1:
                    log_in(2, 2 + len(AHEAD_ROOTS))

            series_of(0)
            log_in(0, 1)
            art_out(0)
            channel_vectors()
            filters()
            series_of(1)
            log_in(1, 2)
            front_norm(0)
            front_factor(0)
            front_y1(0, 0)
            stats(y1, st1, mv1, ve1, 0, "y1_done", T, "st1_done", "mv1_done", "ve1_done")
            art_out(1)
            front_bias(0)
            dve.wait_ge(S["small_hi_done"], 1)
            dve.tensor_tensor(small_lo[:], small_st[:], small_hi[:].bitcast(F32), ALU.subtract).then_inc(S["small_lo_done"], 1)
            conv_low(1, 1, filt[:, 0, :, :])
            conv_low(0, 3, w2_st[:, 1:TAPS:2, :])
            front_x1lo(0, 0)
            conv_low(2, 2, filt[:, 1, :, :])
            dve.wait_ge(S["gru_hi_done"], 1)
            dve.tensor_tensor(gru_lo[:], gru_st[:], gru_hi[:].bitcast(F32), ALU.subtract).then_inc(S["gru_lo_done"], 1)
            step(0, 0, first=True)
            step(1, 1)
            step(2, 0)
            with dve.Fori(3, B - 1, 2) as b:
                step(b, 1)
                step(b + 1, 0)
            step(B - 1, 1, front=False)
            tail_bias(B - 2)
            for part in PARTS:
                tail_r(B - 1, part)
            for part in PARTS:
                tail_n(B - 1, part)
            for part in PARTS:
                c = columns(part)
                dve.wait_ge(S["nn_done"], at(B - 1, 1, part[2]))
                dve.tensor_tensor(xd[:, c], x1t[1][:, c], nn[:, c], ALU.subtract).then_inc(S["xd_done"], 1)
                tail_o(B - 1, part)
            dve.wait_ge(S["out_done"], at(B - 2, T, T))
            for part, bank in zip(PARTS, (bank_w, bank_v)):
                tail_y2(B - 1, 1, part, bank)
                tail_stats(B - 1, part)
            for part in PARTS:
                tail_bias(B - 1, part)

        @block.tensor
        def _(pe):
            def passes(out_ap, w_hi, w_lo, v_hi, v_lo, start=True, stop=True):
                pe.matmul(out_ap, w_hi, v_hi, start=start, stop=False)
                pe.matmul(out_ap, w_lo, v_hi, start=False, stop=False)
                return pe.matmul(out_ap, w_hi, v_lo, start=False, stop=stop)

            def front_support(n, par, loaded):
                pe.wait_ge(S[f"adj_in{par}"], loaded)
                pe.wait_ge(S["xt_done"], n + 1)
                for t in range(T):
                    last = pe.matmul(bank_p[:], xt[:, t, :], adj_sb[par][:, t, :], start=t == 0, stop=t == T - 1)
                last.then_inc(S["supp_mm"], 1)

            def front_rows(n):
                pe.wait_ge(S["supp_out"], n + 1)
                for t in range(T):
                    last = pe.transpose(bank_x[:, t * 128:(t + 1) * 128], supp[:, t * 128:(t + 1) * 128], ident[:])
                last.then_inc(S["srow_mm"], 1)

            def front_x1t(n, par):
                for t in range(T):
                    pe.wait_ge(S["x1_done"], at(n, T, t + 1))
                    last = pe.transpose(bank_x[:, t * 128:(t + 1) * 128], x1_rows[par][:, t, :], ident[:])
                last.then_inc(S["x1t_mm"], 1)

            def tail_rows(t, part=WHOLE, bank=bank_w):
                pe.wait_ge(S["o_done"], at(t, 1, part[2]))
                for k in range(part[0], part[1]):
                    last = pe.transpose(bank[:, k * 128:(k + 1) * 128], o[:, k * 128:(k + 1) * 128], ident[:])
                last.then_inc(S["out_mm"], 1)

            def conv_part(b, p, which):
                out_ap = (bank_p[:, 0:COMMON], bank_c[:, 0:HALF], bank_c[:, HALF:N])[p]
                signal = (2, 0, 1)[p]
                taps, columns = (HT - 1, COMMON) if p == 0 else (HT, HALF)
                w = conv_lo if which == 1 else conv_hi
                v = h_lo if which == 2 else h_hi
                for s in range(taps):
                    last = pe.matmul(out_ap, w[:, p, s, :], v[:, signal, s:s + columns],
                                     start=which == 0 and s == 0, stop=which == 2 and s == taps - 1)
                return last

            def dist(b, t):
                pe.matmul(bank_a[t % 2][:], da[:, t * 128:(t + 1) * 128], db[:], start=True, stop=True
                          ).then_inc(S["dist_mm"], 1)

            def gate(out_ap, g, src, v_hi, v_lo, start, stop):
                return passes(out_ap, gru_hi[:, 3 * src + g, :], gru_lo[:, 3 * src + g, :], v_hi, v_lo, start, stop)

            def step(b, par, first=False, front=True, loaded=None):
                n, t = b + 1, b - 1
                xh, xl = x1t_hi[par], x1t_lo[par]
                pe.wait_ge(S["x1t_out"], at(b, 2, 2))
                pe.wait_ge(S["x1t_lo_done"], b + 1)
                passes(bank_x[:], small_hi[:, 0, :], small_lo[:, 0, :], xh[:], xl[:]).then_inc(S["conv1_done"], 1)
                if not first:
                    pe.wait_ge(S["nm_lo_done"], b)
                passes(bank_y[:], small_hi[:, 1, :], small_lo[:, 1, :], xh[:], xl[:]).then_inc(S["se_done"], 1)
                if not first:
                    pe.wait_ge(S["msgv_done"], b)
                for k in range(T):
                    tile = slice(k * 128, (k + 1) * 128)
                    ins = passes(bank_w[:, tile], xh[:, tile], xl[:, tile], small_hi[:, 2, :], small_lo[:, 2, :])
                ins.then_inc(S["msg_mm"], 1)
                if front:
                    if not first:
                        pe.wait_ge(S["npre_done"], b)
                    front_support(n, 1 - par, loaded)
                if first:
                    pe.wait_ge(S["conv_lo_done"], 3)
                pe.wait_ge(S["hlo_done"], b + 1)
                conv_part(b, 1, 0)
                conv_part(b, 1, 1)
                if not front:
                    conv_part(b, 1, 2)
                    conv_part(b, 2, 0)
                pe.wait_ge(S["dadb_done"], b + 1)
                if not first:
                    pe.wait_ge(S["tr_done"], b)
                dist(b, 0)
                if not first:
                    pe.wait_ge(S["tz_done"], b)
                dist(b, 1)
                if front:
                    pe.wait_ge(S["hhi_done"], b + 1)
                    front_rows(n)
                    conv_part(b, 1, 2)
                if not first:
                    pe.wait_ge(S["msgv_done"], b + 1)
                    tail_rows(t)
                if front:
                    conv_part(b, 2, 0)
                for k in (2, 3):
                    pe.wait_ge(S["exp_done"], at(b, T, k - 1))
                    dist(b, k)
                conv_part(b, 2, 1)
                conv_part(b, 2, 2)
                if not front:
                    pe.wait_ge(S["npre_done"], b)
                pe.wait_ge(S["slo_done"], b + 1)
                conv_part(b, 0, 0)
                conv_part(b, 0, 1)
                conv_part(b, 0, 2).then_inc(S["conv2_done"], 1)
                pe.wait_ge(S["q_done"], b + 1)
                pe.wait_ge(S["msglo_done"], b + 1)
                for k in range(T):
                    pe.wait_ge(S["amlo_done"], at(b, T, k + 1))
                    ins = passes(bank_y[:], msg_hi[:, k, :], msg_lo[:, k, :], am_hi[:, k, :], am_lo[:, k, :],
                                 start=k == 0, stop=k == T - 1)
                ins.then_inc(S["nmp_mm"], 1)
                if first:
                    pe.wait_ge(S["gru_lo_done"], 1)
                pe.wait_ge(S["exp_done"], at(b, T, 4))
                gate(bank_a[0][:], 0, 0, xh[:], xl[:], True, False)
                gate(bank_a[1][:], 1, 0, xh[:], xl[:], True, False)
                if front:
                    front_x1t(n, 1 - par)
                if not first:
                    pe.wait_ge(S["ghn_done"], b)
                gate(bank_v[:], 2, 0, xh[:], xl[:], True, True).then_inc(S["ghn_mm"], 1)
                pe.wait_ge(S["cv_done"], b + 1)
                pe.wait_ge(S["xc_lo_done"], b + 1)
                gate(bank_a[0][:], 0, 1, xc_hi[:], xc_lo[:], False, False)
                gate(bank_p[:], 2, 1, xc_hi[:], xc_lo[:], True, False)
                gate(bank_a[1][:], 1, 1, xc_hi[:], xc_lo[:], False, False)
                pe.wait_ge(S["nm_lo_done"], b + 1)
                gate(bank_a[0][:], 0, 2, nm_hi[:], nm_lo[:], False, True).then_inc(S["r_mm"], 1)
                gate(bank_p[:], 2, 2, nm_hi[:], nm_lo[:], False, True).then_inc(S["n_mm"], 1)
                gate(bank_a[1][:], 1, 2, nm_hi[:], nm_lo[:], False, True).then_inc(S["z_mm"], 1)

            def keep_clock(count):
                for _ in range(count):
                    pe.matmul(bank_v[:], zeros[:, 0:128], zeros[:], start=True, stop=True)

            pe.wait_ge(S["zeros_done"], 1)
            keep_clock(WARM_UP[0])
            front_support(0, 0, 16)
            pe.wait_ge(S["prep_ident"], 16)
            front_rows(0)
            keep_clock(WARM_UP[1])
            front_x1t(0, 0)
            keep_clock(WARM_UP[2])
            pe.wait_ge(S["small_lo_done"], 1)
            pe.wait_ge(S["pad_done"], 3)
            step(0, 0, first=True, loaded=16)
            with pe.Fori(1, B - 1, 2) as b:
                step(b, 1, loaded=8 * b + 24)
                step(b + 1, 0, loaded=8 * b + 24)
            step(B - 1, 1, front=False)
            for part, bank in zip(PARTS, (bank_w, bank_v)):
                tail_rows(B - 1, part, bank)


def kernel(**inputs):
    import numpy as _np
    import concourse.bacc as _bacc
    from concourse import mybir as _mybir
    from concourse.bass_utils import run_bass_kernel_spmd as _run

    g = {k.removeprefix("L1_gnn_"): _np.asarray(v) for k, v in inputs.items()}
    se = _np.zeros((D, 128), _np.float32)
    b_se = _np.zeros(128, _np.float32)
    for group in range(4):
        for kind in range(3):
            at = 32 * group + SE * kind
            se[:, at:at + SE] = g["w_se"].T
            b_se[at:at + SE] = g["b_se"]
    gates = [g["w_hh"].T, g["w_ih"].T[0:D], g["w_ih"].T[D:2 * D]]
    arrays = {
        "x": g["x"],
        "adj_t": g["adj"].transpose(0, 2, 1),
        "w_conv2": g["conv2_w"].transpose(1, 2, 0),
        "w_gru": _np.stack([w[:, D * k:D * (k + 1)] for w in gates for k in range(3)], axis=1),
        "w_small": _np.stack([g["conv1_w"][:, :, 0].T, se, g["w_msg"].T], axis=1),
        "vectors": _np.stack([g["bn1_g"], g["bn1_b"], g["bn1_m"], g["bn1_v"], g["bn2_g"], g["bn2_b"], g["bn2_m"],
                              g["bn2_v"], *g["b_ih"].reshape(3, D), *g["b_hh"].reshape(3, D), b_se], axis=1),
        "b_msg": g["b_msg"],
        "rows_const": distance_rows(),
        "ident_in": _np.eye(128, dtype=_np.float32),
    }
    arrays = {k: _np.ascontiguousarray(v) for k, v in arrays.items()}
    nc = _bacc.Bacc("TRN2", target_bir_lowering=False, num_devices=1)
    args = [nc.dram_tensor(f"in_{k}", a.shape, _mybir.dt.from_np(a.dtype), kind="ExternalInput").ap()
            for k, a in arrays.items()]
    args.append(nc.dram_tensor("out_0", (B, N, D), _mybir.dt.float32, kind="ExternalOutput").ap())
    build(nc, *args)
    r = _run(nc, [{f"in_{k}": a for k, a in arrays.items()}], core_ids=[0])
    return r.results[0]["out_0"]
```
